# Optimizing a Trainium2 kernel written in Bass

```python
import numpy as np
import jax
import jax.numpy as jnp

def _softmax(x, axis=-1):
    return jax.nn.softmax(x, axis=axis)

def _gelu(x):
    return jax.nn.gelu(x, approximate=True)

def _silu(x):
    return jax.nn.silu(x)

def _sigmoid(x):
    return jax.nn.sigmoid(x)

def _layernorm(x, axis=-1, eps=1e-05):
    m = jnp.mean(x, axis=axis, keepdims=True)
    v = jnp.var(x, axis=axis, keepdims=True)
    return (x - m) / jnp.sqrt(v + eps)

def _scatter_add(tgt, idx, src, axis=0):
    return tgt.at[idx].add(src)

def _segment_sum(src, seg, n):
    return jax.ops.segment_sum(src, seg, n)
kernel_name = 'mk_prb_d1_jaxref_r8_47fc06'

def setup_inputs(seed: int=0):
    np.random.seed(seed)
    _w = jnp.asarray

    def _L0_attn_setup():
        import jax, jax.numpy as jnp
        import numpy as np
        import math
        H = 256
        NH = 16
        HD = H // NH
        LAT = 64
        B, S = (2, 256)
        ROPE_DIM = H // 4

        def _rope_cos_sin(seq_len, dim, base=10000.0):
            inv_freq = 1.0 / base ** (jnp.arange(0, dim, 2, dtype=jnp.float32) / dim)
            t = jnp.arange(seq_len, dtype=jnp.float32)
            freqs = jnp.outer(t, inv_freq)
            emb = jnp.concatenate([freqs, freqs], -1)
            return (jnp.cos(emb), jnp.sin(emb))

        def _apply_rotary(x, cos, sin):
            h = x.shape[-1] // 2
            x1, x2 = (x[..., :h], x[..., h:])
            return jnp.concatenate([x1 * cos - x2 * sin, x1 * sin + x2 * cos], -1)
        key = jax.random.key(seed)
        ks = jax.random.split(key, 8)

        def lin(k, out_d, in_d):
            k1, k2 = jax.random.split(k)
            return (jax.random.normal(k1, (out_d, in_d), jnp.float32) * 0.02, jax.random.normal(k2, (out_d,), jnp.float32) * 0.02)
        Wq_down, bq_down = lin(ks[0], LAT, H)
        Wkv_down, bkv_down = lin(ks[1], LAT, H)
        Wq_up, bq_up = lin(ks[2], H // 2, LAT)
        Wk_up, bk_up = lin(ks[3], H // 2, LAT)
        Wv_up, bv_up = lin(ks[4], H, LAT)
        Wo, bo = lin(ks[5], H, H)
        hidden_states = jax.random.normal(ks[6], (B, S, H), jnp.float32)
        return dict(hidden_states=hidden_states, Wq_down=Wq_down, bq_down=bq_down, Wkv_down=Wkv_down, bkv_down=bkv_down, Wq_up=Wq_up, bq_up=bq_up, Wk_up=Wk_up, bk_up=bk_up, Wv_up=Wv_up, bv_up=bv_up, Wo=Wo, bo=bo)
    _L0_attn_in = _L0_attn_setup()

    def _L0_ffn_setup():
        import jax, jax.numpy as jnp
        import numpy as np
        E, H, I = (8, 256, 512)
        TOP_K = 1
        B, S = (1, 256)
        key = jax.random.key(seed)
        ks = jax.random.split(key, 7)
        std = 0.02
        return {'hidden_states': jax.random.normal(ks[0], (B, S, H), dtype=jnp.float32), 'router_w': jax.random.normal(ks[1], (E, H), dtype=jnp.float32) * std, 'gate_up_proj': jax.random.normal(ks[2], (E, H, 2 * I), dtype=jnp.float32) * std, 'down_proj': jax.random.normal(ks[3], (E, I, H), dtype=jnp.float32) * std, 'shared_gate_w': jax.random.normal(ks[4], (H, I), dtype=jnp.float32) * std, 'shared_up_w': jax.random.normal(ks[5], (H, I), dtype=jnp.float32) * std, 'shared_down_w': jax.random.normal(ks[6], (I, H), dtype=jnp.float32) * std}
    _L0_ffn_in = _L0_ffn_setup()
    _d = {'L0_attn_hidden_states': _L0_attn_in['hidden_states'], 'L0_attn_Wq_down': _L0_attn_in['Wq_down'], 'L0_attn_bq_down': _L0_attn_in['bq_down'], 'L0_attn_Wkv_down': _L0_attn_in['Wkv_down'], 'L0_attn_bkv_down': _L0_attn_in['bkv_down'], 'L0_attn_Wq_up': _L0_attn_in['Wq_up'], 'L0_attn_bq_up': _L0_attn_in['bq_up'], 'L0_attn_Wk_up': _L0_attn_in['Wk_up'], 'L0_attn_bk_up': _L0_attn_in['bk_up'], 'L0_attn_Wv_up': _L0_attn_in['Wv_up'], 'L0_attn_bv_up': _L0_attn_in['bv_up'], 'L0_attn_Wo': _L0_attn_in['Wo'], 'L0_attn_bo': _L0_attn_in['bo'], 'L0_ffn_router_w': _L0_ffn_in['router_w'], 'L0_ffn_gate_up_proj': _L0_ffn_in['gate_up_proj'], 'L0_ffn_down_proj': _L0_ffn_in['down_proj'], 'L0_ffn_shared_gate_w': _L0_ffn_in['shared_gate_w'], 'L0_ffn_shared_up_w': _L0_ffn_in['shared_up_w'], 'L0_ffn_shared_down_w': _L0_ffn_in['shared_down_w']}
    _x0 = _d['L0_attn_hidden_states']
    _d['L0_attn_hidden_states'] = jax.random.normal(jax.random.fold_in(jax.random.key(seed), 1), (1, 1024, 256), dtype=_x0.dtype)
    del _x0
    return _d

def reference(L0_attn_hidden_states, L0_attn_Wq_down, L0_attn_bq_down, L0_attn_Wkv_down, L0_attn_bkv_down, L0_attn_Wq_up, L0_attn_bq_up, L0_attn_Wk_up, L0_attn_bk_up, L0_attn_Wv_up, L0_attn_bv_up, L0_attn_Wo, L0_attn_bo, L0_ffn_router_w, L0_ffn_gate_up_proj, L0_ffn_down_proj, L0_ffn_shared_gate_w, L0_ffn_shared_up_w, L0_ffn_shared_down_w):

    def _L0_attn_ref(hidden_states, Wq_down, bq_down, Wkv_down, bkv_down, Wq_up, bq_up, Wk_up, bk_up, Wv_up, bv_up, Wo, bo):
        import jax, jax.numpy as jnp
        import numpy as np
        import math
        H = 256
        NH = 16
        HD = H // NH
        LAT = 64
        B, S = (2, 256)
        ROPE_DIM = H // 4

        def _rope_cos_sin(seq_len, dim, base=10000.0):
            inv_freq = 1.0 / base ** (jnp.arange(0, dim, 2, dtype=jnp.float32) / dim)
            t = jnp.arange(seq_len, dtype=jnp.float32)
            freqs = jnp.outer(t, inv_freq)
            emb = jnp.concatenate([freqs, freqs], -1)
            return (jnp.cos(emb), jnp.sin(emb))

        def _apply_rotary(x, cos, sin):
            h = x.shape[-1] // 2
            x1, x2 = (x[..., :h], x[..., h:])
            return jnp.concatenate([x1 * cos - x2 * sin, x1 * sin + x2 * cos], -1)
        bsz, seq, _ = hidden_states.shape
        q_lat = hidden_states @ Wq_down.T + bq_down
        kv_lat = hidden_states @ Wkv_down.T + bkv_down
        cos, sin = _rope_cos_sin(seq, ROPE_DIM)
        q_half = q_lat @ Wq_up.T + bq_up
        q = jnp.concatenate([q_half, _apply_rotary(q_half, cos, sin)], -1)
        k_half = kv_lat @ Wk_up.T + bk_up
        k = jnp.concatenate([k_half, _apply_rotary(k_half, cos, sin)], -1)
        v = kv_lat @ Wv_up.T + bv_up
        q = q.reshape(bsz, seq, NH, HD).transpose(0, 2, 1, 3)
        k = k.reshape(bsz, seq, NH, HD).transpose(0, 2, 1, 3)
        v = v.reshape(bsz, seq, NH, HD).transpose(0, 2, 1, 3)
        scores = jnp.einsum('bhqd,bhkd->bhqk', q, k) / math.sqrt(HD)
        attn = jax.nn.softmax(scores, axis=-1)
        out = jnp.einsum('bhqk,bhkd->bhqd', attn, v)
        out = out.transpose(0, 2, 1, 3).reshape(bsz, seq, H)
        return out @ Wo.T + bo

    def _L0_ffn_ref(hidden_states, router_w, gate_up_proj, down_proj, shared_gate_w, shared_up_w, shared_down_w):
        import jax, jax.numpy as jnp
        import numpy as np
        E, H, I = (8, 256, 512)
        TOP_K = 1
        B, S = (1, 256)
        orig_shape = hidden_states.shape
        x = hidden_states.reshape(-1, H)
        T = x.shape[0]
        logits = x @ router_w.T
        top_vals, top_idx = jax.lax.top_k(logits, TOP_K)
        scores = jnp.full_like(logits, -jnp.inf)
        scores = scores.at[jnp.arange(T)[:, None], top_idx].set(top_vals)
        scores = jax.nn.sigmoid(scores.astype(jnp.float32)).astype(logits.dtype)
        xr = x[None, :, :] * scores.T[:, :, None]
        gate_up = jnp.einsum('eth,ehf->etf', xr, gate_up_proj)
        gate, up = jnp.split(gate_up, 2, axis=-1)
        routed = jnp.einsum('etf,efh->eth', up * jax.nn.silu(gate), down_proj)
        routed_sum = routed.sum(axis=0)
        shared = jax.nn.silu(x @ shared_gate_w) * (x @ shared_up_w) @ shared_down_w
        return (shared + routed_sum).reshape(orig_shape)
    x = L0_attn_hidden_states
    xn = _layernorm(x, axis=-1)
    x = x + _L0_attn_ref(xn, L0_attn_Wq_down, L0_attn_bq_down, L0_attn_Wkv_down, L0_attn_bkv_down, L0_attn_Wq_up, L0_attn_bq_up, L0_attn_Wk_up, L0_attn_bk_up, L0_attn_Wv_up, L0_attn_bv_up, L0_attn_Wo, L0_attn_bo) + _L0_ffn_ref(xn, L0_ffn_router_w, L0_ffn_gate_up_proj, L0_ffn_down_proj, L0_ffn_shared_gate_w, L0_ffn_shared_up_w, L0_ffn_shared_down_w)
    return x

_drawn_inputs = setup_inputs


def setup_inputs(seed=0):
    import zlib

    import numpy as np

    out = dict(_drawn_inputs(seed))
    spreads = {}
    factors = {'L0_attn_Wq_down': 8.0,
     'L0_attn_bq_down': 8.0,
     'L0_attn_Wkv_down': 8.0,
     'L0_attn_bkv_down': 8.0,
     'L0_attn_Wq_up': 8.0,
     'L0_attn_bq_up': 8.0,
     'L0_attn_Wk_up': 8.0,
     'L0_attn_bk_up': 8.0,
     'L0_attn_Wv_up': 8.0,
     'L0_attn_bv_up': 22.206,
     'L0_attn_Wo': 8.0,
     'L0_attn_bo': 23.568,
     'L0_ffn_router_w': 6.565,
     'L0_ffn_gate_up_proj': 6.117,
     'L0_ffn_down_proj': 6.1,
     'L0_ffn_shared_gate_w': 8.0,
     'L0_ffn_shared_up_w': 8.0,
     'L0_ffn_shared_down_w': 8.0}
    for name, (base, spread) in spreads.items():
        noise = np.random.default_rng([zlib.crc32(name.encode()), seed]).standard_normal(out[name].shape)
        drawn = base * np.exp(spread * noise) if base else spread * noise
        out[name] = jnp.asarray(drawn.astype(out[name].dtype))
    for name, factor in factors.items():
        out[name] = (out[name] * factor).astype(out[name].dtype)
    return out
```

```python
from contextlib import ExitStack

import numpy as np

import concourse.bass as bass
from concourse import mybir

F32 = mybir.dt.float32
BF16 = mybir.dt.bfloat16
I32 = mybir.dt.int32
ALU = mybir.AluOpType
ACT = mybir.ActivationFunctionType
AX = mybir.AxisListType

P = 128
T, H = 1024, 256
NH, HD, LAT = 16, 16, 64
E, F = 8, 512
EPS = 1e-5
NT = T // P
KH, KF = H // P, F // P
GH = 4
NG = NH // GH
HALF = T // 2
STRIP = P // GH
PARTS_Q = (0, 0, 1, 1, 0, 2)
PARTS_K = (0, 1, 0, 1, 2, 0)
KROWS = len(PARTS_Q) * HD
ROWS = KROWS + 3
TILES = T // P + E - 1
GU = 2 * F
WEXP = KH * GU + KF * H

Q_WORDS = 2 * NH * HALF // 2
K_WORDS = NH * T // 2
STACKS_AT = (E // 2) * WEXP
ARENA = STACKS_AT + Q_WORDS + K_WORDS


def build_kernel(nc, x, lat_w, lat_b, up_w, up_b, v_w, v_b, rope_c, rope_s, router_w, sgu_w, sdn_w,
                 out_w, out_b, gate_up, down, consts, one_rows, out):
    nc.disable_value_cache = True
    ctx = ExitStack()
    with ctx:
        def sb(name, shape, dt=F32):
            return ctx.enter_context(nc.sbuf_tensor(name, shape, dt))

        def sem(name):
            return ctx.enter_context(nc.semaphore(name))

        ps = ctx.enter_context(nc.psum_tensor("ps", [P, 8, 512], F32))

        part_dram = [nc.dram_tensor(f"parts_{s}", [3, 2, P, T], BF16, kind="Internal").ap() for s in "qk"]
        sorted_x = nc.dram_tensor("sorted_x", [TILES * P, H], F32, kind="Internal").ap()
        sorted_y = nc.dram_tensor("sorted_y", [TILES * P, H], F32, kind="Internal").ap()

        arena = sb("arena", [P, ARENA])
        resid = sb("resid", [P, NT, H])
        xn = sb("xn", [P, NT, H])
        v_all = sb("v_all", [P, NG, NT, GH, HD])
        v_group = sb("v_group", [P, NT, GH, STRIP])
        probs = sb("probs", [P, 2, GH, HALF])
        attn = sb("attn", [P, NG, T])
        hid = sb("hid", [P, KF, T])
        acc_sb = sb("acc_sb", [P, 2, HALF])
        rden = sb("rden", [P, 2, HALF])
        cst = sb("cst", [P, 2 * P + 3 * 64 + TILES * E])
        ident_bf = sb("ident_bf", [P, P], BF16)
        before_bf = sb("before_bf", [P, P], BF16)
        ones_bf = sb("ones_bf", [P, P], BF16)
        lat_bias = sb("lat_bias", [P, 1])
        up_bias = sb("up_bias", [P, 4])
        stats = sb("stats", [P, NT, 6])
        mv = sb("mv", [P, NT, 2])
        veps = sb("veps", [P, NT])
        minus_half = sb("minus_half", [P, NT])
        rstd = sb("rstd", [P, NT])
        token_pool = sb("token_pool", [P, 2])
        wait_slot = sb("wait_slot", [P, 1])
        token_act = sb("token_act", [P, 4])
        negmax = sb("negmax", [P, 2, GH * 4])
        split1 = sb("split1", [P, GH * 4])
        split2 = sb("split2", [P, GH * 4])
        negmax_parts = sb("negmax_parts", [P, P], BF16)
        negmax_rows = sb("negmax_rows", [3 * GH * 4, P], BF16)
        tile_exp_i = sb("tile_exp_i", [P, TILES], I32)
        dest_i = sb("dest_i", [P, NT], I32)
        esc = sb("esc", [P, NT])
        esc1 = sb("esc1", [P, NT])
        score = sb("score", [P, NT])

        def words(at, n):
            return arena[:, at:at + n]

        q_stack = words(STACKS_AT, Q_WORDS).bitcast(BF16).rearrange("p (c h t) -> p c h t", c=2, h=NH)
        k_stack = words(STACKS_AT + Q_WORDS, K_WORDS).bitcast(BF16).rearrange("p (h t) -> p h t", h=NH)
        exp_w = words(0, E * WEXP).rearrange("p (e n) -> p e n", e=E)
        at = 0

        def temp(n):
            nonlocal at
            at += n
            return words(at - n, n)

        cos_t, sin_t = temp(T), temp(T)
        qk_f = temp(2 * HALF).rearrange("p (h t) -> p h t", h=2)
        rot_a, rot_b = temp(HALF), temp(HALF)
        res1 = temp(2 * HALF).rearrange("p (h t) -> p h t", h=2)
        res2 = temp(2 * HALF).rearrange("p (h t) -> p h t", h=2)
        parts = temp(2 * 3 * T // 2 * 2 // 2 * 1).bitcast(BF16).rearrange(
            "p (b a h t) -> p b a h t", b=2, a=3, h=2)
        lat = temp(T)
        logit_t = cos_t
        lat_wt = temp(KH * P).rearrange("p (k n) -> p k n", k=KH)
        up_wt = temp(2 * P)
        v_wt = temp(H)
        v_bias = temp(H)
        out_bias = temp(H)
        router_t = temp(KH * E).rearrange("p (k e) -> p k e", k=KH)
        te = "p (t e) -> p t e"
        lg, pick, pick2, onehot = [temp(NT * E).rearrange(te, t=NT) for _ in range(4)]
        top, pickmax, dest = temp(NT), temp(NT), temp(NT)
        onehot_bf = temp(NT * E // 2).bitcast(BF16)
        ranks = temp(2 * NT * E).rearrange("p (a t e) -> p a t e", a=2, t=NT)
        passed = temp((NT + 1) * E).rearrange(te, e=E)
        cmp3 = temp(E * E).rearrange("p (e m) -> p e m", e=E)
        tiles_of, start_of, end_of = temp(E), temp(E), temp(E)
        cmpj = temp(TILES * E).rearrange(te, e=E)
        tile_exp = temp(TILES)
        assert at <= STACKS_AT, at

        v_words = v_all[:, :, :, :, :].rearrange("p g t j d -> p (g t j d)")
        sdn = v_words[:, 0:KF * H].rearrange("p (k n) -> p k n", k=KF)
        wout = v_words[:, KF * H:KF * H + NG * H].rearrange("p (g n) -> p g n", g=NG)

        attn_w = attn[:, :, :].rearrange("p g t -> p (g t)")
        x_t = attn_w[:, 0:KH * T].rearrange("p (k t) -> p k t", k=KH)
        sgu = attn_w[:, KH * T:KH * T + KH * GU].rearrange("p (k n) -> p k n", k=KH)
        gathered = attn_w[:, 0:NT * H].rearrange("p (t n) -> p t n", t=NT)
        probs_w = probs[:, :, :, :].rearrange("p a j t -> p (a j t)")
        sh_gate = [probs_w[:, 1024 * u:1024 * u + 512] for u in range(2)]
        sh_up = [probs_w[:, 1024 * u + 512:1024 * u + 1024] for u in range(2)]
        tile_x = probs_w[:, 0:256]
        tile_xt = probs_w[:, 256:512].rearrange("p (k t) -> p k t", k=KH)
        tile_gate = probs_w[:, 512:1024]
        tile_h = probs_w[:, 1024:1536]
        tile_ht = probs_w[:, 1536:2048].rearrange("p (k t) -> p k t", k=KF)
        tile_y = probs_w[:, 2048:2304]

        ident = cst[:, 0:P]
        before = cst[:, P:2 * P]
        c0 = 2 * P
        weight_of = cst[:, c0:c0 + 64].rearrange("p (t e) -> p t e", t=NT)
        steps_128 = cst[:, c0 + 64:c0 + 128].rearrange("p (e m) -> p e m", e=E)
        earlier = cst[:, c0 + 128:c0 + 192].rearrange("p (e m) -> p e m", e=E)
        tile_no = cst[:, c0 + 192:c0 + 192 + TILES * E].rearrange("p (j e) -> p j e", j=TILES)

        x_in = [sem(f"x_in{i}") for i in range(4)]
        consts_in, latw_in, upw_in, rope_in = sem("consts_in"), sem("latw_in"), sem("upw_in"), sem("rope_in")
        vw_in, router_in, sgu_in, tail_in = sem("vw_in"), sem("router_in"), sem("sgu_in"), sem("tail_in")
        stats_ready, mv_ready, veps_ready = sem("stats_ready"), sem("mv_ready"), sem("veps_ready")
        rstd_ready, half_set = sem("rstd_ready"), sem("half_set")
        xn_ready, xt_psum, xt_ready_a, xt_ready_v = sem("xn_ready"), sem("xt_psum"), sem("xt_ready_a"), sem("xt_ready_v")
        casts_ready, ones_ready = sem("casts_ready"), sem("ones_ready")
        lat_psum, lat_ready = sem("lat_psum"), sem("lat_ready")
        up_psum, up_read, qk_ready = sem("up_psum"), sem("up_read"), sem("qk_ready")
        rot_step, high_ready, res1_ready, mid_ready = sem("rot_step"), sem("high_ready"), sem("res1_ready"), sem("mid_ready")
        res2_ready, low_ready = sem("res2_ready"), sem("low_ready")
        parts_stored = [sem(f"parts_stored_{i}") for i in range(4)]
        stacks_in = [sem(f"stacks_in{i}") for i in range(3)]
        v_psum, v_ready = sem("v_psum"), sem("v_ready")
        lgt_psum, lgt_ready, lg_psum, lg_ready = sem("lgt_psum"), sem("lgt_ready"), sem("lg_psum"), sem("lg_ready")
        route_step, onehot_ready, rank_psum, ranks_ready = sem("route_step"), sem("onehot_ready"), sem("rank_psum"), sem("ranks_ready")
        top_ready, esc_ready, score_ready, dest_ready = sem("top_ready"), sem("esc_ready"), sem("score_ready"), sem("dest_ready")
        scaled_ready, zero_set, zeros_in, scattered = sem("scaled_ready"), sem("zero_set"), sem("zeros_in"), sem("scattered")
        bias_added = sem("bias_added")
        gu_psum, gu_read, up_copied, hid_ready = sem("gu_psum"), sem("gu_read"), sem("up_copied"), sem("hid_ready")
        max_scores, max_read = sem("max_scores"), sem("max_read")
        split_step, negmax_split, negmax_turned = sem("split_step"), sem("negmax_split"), sem("negmax_turned")
        negmax_copied, negmax_in = sem("negmax_copied"), sem("negmax_in")
        scores_psum, probs_ready, probs_used = sem("scores_psum"), sem("probs_ready"), sem("probs_used")
        acc_read, den_ready, rden_ready, attn_ready = sem("acc_read"), sem("den_ready"), sem("rden_ready"), sem("attn_ready")
        vg_ready = sem("vg_ready")
        exp_low_in, exp_high_in = sem("exp_low_in"), sem("exp_high_in")
        token_psum, token_summed = sem("token_psum"), sem("token_summed")
        tile_in, tile_turned, tile_xt_ready = sem("tile_in"), sem("tile_turned"), sem("tile_xt_ready")
        tile_gu_psum, tile_gate_ready, tile_h_ready = sem("tile_gu_psum"), sem("tile_gate_ready"), sem("tile_h_ready")
        tile_ht_psum, tile_ht_ready, tile_y_psum = sem("tile_ht_psum"), sem("tile_ht_ready"), sem("tile_y_psum")
        tile_y_ready, tile_out = sem("tile_y_ready"), sem("tile_out")
        gathered_in, final_ready, stored = sem("gathered_in"), sem("final_ready"), sem("stored")

        x_dram = x.rearrange("(t p) d -> p t d", p=P)
        out_dram = out.rearrange("(t p) d -> p t d", p=P)

        def q_part(a, g, c):
            rows = slice((g % 2) * GH * HD, (g % 2 + 1) * GH * HD)
            return part_dram[0][a, g // 2, rows, c * HALF:(c + 1) * HALF].rearrange("(h d) t -> d h t", d=HD)

        def k_part(a, g):
            rows = slice((g % 2) * GH * HD, (g % 2 + 1) * GH * HD)
            return part_dram[1][a, g // 2, rows, :].rearrange("(h d) t -> d h t", d=HD)

        block = ctx.enter_context(nc.Block())

        @block.sync
        def _(sp):
            sp.dma_start(resid[:, 0:2, :], x_dram[:, 0:2, :]).then_inc(x_in[0], 16)
            sp.dma_start(resid[:, 4:6, :], x_dram[:, 4:6, :]).then_inc(x_in[2], 16)
            sp.dma_start(cst[:, :], consts).then_inc(consts_in, 16)
            sp.dma_start(lat_wt, lat_w.rearrange("(p k) n -> p k n", k=KH)).then_inc(latw_in, 16)
            sp.dma_start(lat_bias[:, :], lat_b).then_inc(latw_in, 16)
            sp.dma_start(up_wt, up_w).then_inc(upw_in, 16)
            sp.dma_start(up_bias[:, :], up_b).then_inc(upw_in, 16)
            sp.dma_start(k_stack[KROWS:ROWS, :, :], one_rows).then_inc(upw_in, 16)
            sp.dma_start(router_t, router_w.rearrange("(p k) e -> p k e", k=KH)).then_inc(router_in, 16)

            for i in range(4):
                s, c = i % 2, i // 2
                sp.wait_ge(low_ready, i + 1)
                sp.wait_ge(mid_ready, i + 1)
                sp.wait_ge(high_ready, i + 1)
                for a in range(3):
                    sp.dma_start(part_dram[s][a, :, :, c * HALF:(c + 1) * HALF].rearrange("h p t -> p h t"),
                                 parts[:, i % 2, a, :, :]).then_inc(parts_stored[i], 16)
            for i in range(4):
                sp.wait_ge(parts_stored[i], 48)
            for n, groups in enumerate(((0,), (1,), (2, 3))):
                for g in groups:
                    hs = slice(GH * g, GH * g + GH)
                    for b in range(len(PARTS_Q)):
                        rows = slice(HD * b, HD * b + HD)
                        sp.dma_start(k_stack[rows, hs, :], k_part(PARTS_K[b], g)).then_inc(stacks_in[n], 16)
                        for c in range(2):
                            sp.dma_start(q_stack[rows, c, hs, :], q_part(PARTS_Q[b], g, c)).then_inc(stacks_in[n], 16)
            sp.wait_ge(v_ready, NT)
            sp.wait_ge(lg_psum, NT)
            sp.wait_ge(bias_added, NT)
            sp.wait_ge(dest_ready, 1)
            for e in range(E // 2):
                sp.dma_start(exp_w[:, e, 0:KH * GU], gate_up[e].rearrange("(p k) n -> p (k n)", k=KH)).then_inc(exp_low_in, 16)
                sp.dma_start(exp_w[:, e, KH * GU:], down[e].rearrange("(p k) n -> p (k n)", k=KF)).then_inc(exp_low_in, 16)

            def negmax_load(m, g, c):
                sp.wait_ge(negmax_copied, m + 1)
                for a in range(3):
                    sp.dma_start(q_stack[KROWS + a:KROWS + a + 1, c, bass.ds(GH * g, GH), :].rearrange("p h t -> p (h t)"),
                                 negmax_rows[16 * a:16 * a + 16, :]).then_inc(negmax_in, 16)

            negmax_load(0, 0, 0)
            with sp.Fori(0, NG - 1) as g:
                negmax_load(2 * g + 1, g, 1)
                negmax_load(2 * g + 2, g + 1, 0)
            negmax_load(2 * NG - 1, NG - 1, 1)
            sp.wait_ge(vg_ready, NT * NG)
            sp.dma_start(sdn, sdn_w.rearrange("(p k) n -> p k n", k=KF)).then_inc(tail_in, 16)
            sp.dma_start(wout, out_w).then_inc(tail_in, 16)

            sp.wait_ge(scores_psum, NH * NT * 2)
            for e in range(E // 2, E):
                sp.dma_start(exp_w[:, e, 0:KH * GU], gate_up[e].rearrange("(p k) n -> p (k n)", k=KH)).then_inc(exp_high_in, 16)
                sp.dma_start(exp_w[:, e, KH * GU:], down[e].rearrange("(p k) n -> p (k n)", k=KF)).then_inc(exp_high_in, 16)

            sp.wait_ge(scattered, 16 * NT)
            sp.wait_ge(probs_used, 2 + 8 * NT)
            sp.dma_start(tile_x, sorted_x[0:P, :]).then_inc(tile_in, 16)
            with sp.Fori(1, TILES) as i:
                sp.wait_ge(tile_turned, i)
                sp.dma_start(tile_x, sorted_x[bass.ds(i * P, P), :]).then_inc(tile_in, 16)

            for t in range(NT):
                sp.wait_ge(final_ready, t + 1)
                sp.dma_start(out_dram[:, t, :], resid[:, t, :]).then_inc(stored, 16)
            sp.wait_ge(stored, 16 * NT)

        @block.scalar
        def _(act):
            act.dma_start(resid[:, 2:4, :], x_dram[:, 2:4, :]).then_inc(x_in[1], 16)
            act.dma_start(resid[:, 6:8, :], x_dram[:, 6:8, :]).then_inc(x_in[3], 16)
            act.dma_start(cos_t, rope_c).then_inc(rope_in, 16)
            act.dma_start(sin_t, rope_s).then_inc(rope_in, 16)
            act.dma_start(v_wt, v_w).then_inc(vw_in, 16)
            act.dma_start(v_bias, v_b.partition_broadcast(P)).then_inc(vw_in, 16)
            act.dma_start(out_bias, out_b.partition_broadcast(P)).then_inc(vw_in, 16)
            act.dma_start(sgu, sgu_w.rearrange("(p k) n -> p k n", k=KH)).then_inc(sgu_in, 16)

            for hf in range(2):
                act.wait_ge(xt_psum, 2 * hf + 1)
                nc.scalar.copy(x_t[:, 0, hf * HALF:(hf + 1) * HALF], ps[:, 2 * hf, :]).then_inc(xt_ready_a, 1)
            act.wait_ge(latw_in, 32)
            for c in range(2):
                act.wait_ge(lat_psum, c + 1)
                nc.scalar.activation(lat[:, c * HALF:(c + 1) * HALF], ps[:, 4 + c, :], ACT.Identity,
                                     bias=lat_bias[:, 0:1]).then_inc(lat_ready, 1)
            for i in range(4):
                act.wait_ge(qk_ready, i + 1)
                if i >= 2:
                    act.wait_ge(parts_stored[i - 2], 48)
                nc.scalar.copy(parts[:, i % 2, 0], qk_f).then_inc(high_ready, 1)
                act.wait_ge(res1_ready, i + 1)
                nc.scalar.copy(parts[:, i % 2, 1], res1).then_inc(mid_ready, 1)
                act.wait_ge(res2_ready, i + 1)
                nc.scalar.copy(parts[:, i % 2, 2], res2).then_inc(low_ready, 1)
            for c in range(2):
                act.wait_ge(lgt_psum, c + 1)
                nc.scalar.copy(logit_t[0:E, c * HALF:(c + 1) * HALF], ps[0:E, 4 + c, :]).then_inc(lgt_ready, 1)
            act.wait_ge(top_ready, 1)
            nc.scalar.activation(esc[:, :], top, ACT.Exp, scale=-1.0).then_inc(esc_ready, 1)

            act.wait_ge(zeros_in, 16)
            for u in range(8):
                b = 0 if u % 2 == 0 else 6
                act.wait_ge(gu_psum, u + 1)
                if u >= 2:
                    act.wait_ge(hid_ready, u - 1)
                g_op = nc.scalar.activation(sh_gate[u % 2], ps[:, b, :], ACT.Silu)
                g_op.then_inc(gu_read, 1)
                u_op = nc.scalar.copy(sh_up[u % 2], ps[:, b + 1, :])
                u_op.then_inc(gu_read, 1)

            def negmax_copy(m, c):
                act.wait_ge(negmax_turned, m + 1)
                act.wait_ge(negmax_in, 48 * m)
                nc.scalar.copy(negmax_rows[:, :], ps[0:48, 6 + c, 0:64].bitcast(BF16)).then_inc(negmax_copied, 1)

            act.wait_ge(negmax_turned, 1)
            nc.scalar.copy(negmax_rows[:, :], ps[0:48, 6, 0:64].bitcast(BF16)).then_inc(negmax_copied, 1)
            act.wait_ge(hid_ready, 8)
            for i, token in enumerate((probs_ready, probs_ready, acc_read, acc_read)):
                nc.scalar.copy(token_act[:, i:i + 1], esc[:, 0:1]).then_inc(token, 1)

            def half(g, c, negmax):
                m = 2 * g + c
                for kt in range(NT):
                    step = NT * m + kt
                    for j in range(GH):
                        act.wait_ge(scores_psum, GH * step + j + 1)
                        if j == 0:
                            act.wait_ge(probs_used, step + 1)
                        nc.scalar.activation(probs[:, kt % 2, j, :], ps[:, j % 2, :], ACT.Exp,
                                             scale=HD ** -0.5).then_inc(probs_ready, 1)
                    if kt == 3 and negmax:
                        negmax_copy(m + 1, 1 - c)
                act.wait_ge(probs_used, 2 + NT * (m + 1))
                act.wait_ge(attn_ready, m + 1)
                nc.scalar.copy(acc_sb[:, c, :], ps[:, 6 + c, :]).then_inc(acc_read, 1)

            with act.Fori(0, NG - 1) as g:
                half(g, 0, True)
                half(g, 1, True)
            half(NG - 1, 0, True)
            half(NG - 1, 1, False)

            def evacuate(i):
                act.wait_ge(tile_gu_psum, i + 1)
                nc.scalar.activation(tile_gate, ps[:, 0, :], ACT.Silu).then_inc(tile_gate_ready, 1)

            def down_out(i):
                act.wait_ge(tile_y_psum, i + 1)
                if not isinstance(i, int) or i > 0:
                    act.wait_ge(tile_out, 16 * i)
                nc.scalar.copy(tile_y, ps[:, 5, 0:H]).then_inc(tile_y_ready, 1)
                act.wait_ge(tile_y_ready, i + 1)
                act.dma_start(sorted_y[bass.ds(i * P, P), :], tile_y).then_inc(tile_out, 16)

            def ht_copy(i):
                act.wait_ge(tile_ht_psum, i + 1)
                nc.scalar.copy(tile_ht, ps[:, 3, :].rearrange("p (k t) -> p k t", k=KF)).then_inc(tile_ht_ready, 1)

            evacuate(0)
            ht_copy(0)
            evacuate(1)
            down_out(0)
            ht_copy(1)
            with act.Fori(2, TILES) as i:
                evacuate(i)
                down_out(i - 1)
                ht_copy(i)
            down_out(TILES - 1)

        @block.vector
        def _(dve):
            nc.vector.memset(negmax_parts[:, :], 0.0).then_inc(casts_ready, 1)
            dve.wait_ge(consts_in, 16)
            nc.vector.tensor_copy(ident_bf[:, :], ident).then_inc(casts_ready, 1)
            nc.vector.tensor_copy(before_bf[:, :], before).then_inc(casts_ready, 1)
            for hf in range(2):
                for t in range(4 * hf, 4 * hf + 4):
                    if t % 2 == 0:
                        dve.wait_ge(x_in[t // 2], 16)
                    nc.vector.bn_stats(stats[:, t, :], resid[:, t, :]).then_inc(stats_ready, 1)
                for t in range(4 * hf, 4 * hf + 4):
                    dve.wait_ge(stats_ready, t + 1)
                    nc.vector.bn_aggr(mv[:, t, :], stats[:, t, :]).then_inc(mv_ready, 1)
                dve.wait_ge(mv_ready, 4 * hf + 4)
                nc.vector.tensor_scalar(veps[:, 4 * hf:4 * hf + 4], mv[:, 4 * hf:4 * hf + 4, 1], EPS, None,
                                        ALU.add).then_inc(veps_ready, 1)
            for hf in range(2):
                dve.wait_ge(rstd_ready, hf + 1)
                for t in range(4 * hf, 4 * hf + 4):
                    nc.vector.tensor_scalar(xn[:, t, :], resid[:, t, :], mv[:, t, 0:1], rstd[:, t:t + 1],
                                            ALU.subtract, ALU.mult).then_inc(xn_ready, 1)
            for hf in range(2):
                dve.wait_ge(xt_psum, 2 * hf + 2)
                nc.vector.tensor_copy(x_t[:, 1, hf * HALF:(hf + 1) * HALF], ps[:, 2 * hf + 1, :]).then_inc(xt_ready_v, 1)
            dve.wait_ge(upw_in, 48)
            dve.wait_ge(rope_in, 32)
            for i in range(4):
                s, c = i % 2, i // 2
                b = 4 * c + 2 * s
                tt = slice(c * HALF, (c + 1) * HALF)
                dve.wait_ge(up_psum, i + 1)
                if i >= 1:
                    dve.wait_ge(high_ready, i)
                nc.vector.tensor_scalar(qk_f[:, 0, :], ps[:, b, :], up_bias[:, 2 * s:2 * s + 1], None, ALU.add)\
                    .then_inc(rot_step, 1)
                nc.vector.scalar_tensor_tensor(rot_a, ps[:, b, :], up_bias[:, 2 * s:2 * s + 1], cos_t[:, tt],
                                               ALU.add, ALU.mult).then_inc(rot_step, 1)
                nc.vector.scalar_tensor_tensor(rot_b, ps[:, b + 1, :], up_bias[:, 2 * s + 1:2 * s + 2], sin_t[:, tt],
                                               ALU.add, ALU.mult).then_inc(up_read, 1)
                dve.wait_ge(rot_step, 2 * i + 2)
                dve.wait_ge(up_read, i + 1)
                nc.vector.tensor_tensor(qk_f[:, 1, :], rot_a, rot_b, ALU.add).then_inc(qk_ready, 1)
                dve.wait_ge(high_ready, i + 1)
                nc.vector.tensor_tensor(res1, qk_f, parts[:, i % 2, 0], ALU.subtract).then_inc(res1_ready, 1)
                dve.wait_ge(mid_ready, i + 1)
                if i >= 1:
                    dve.wait_ge(low_ready, i)
                nc.vector.tensor_tensor(res2, res1, parts[:, i % 2, 1], ALU.subtract).then_inc(res2_ready, 1)
            dve.wait_ge(vw_in, 48)
            for t in range(NT):
                dve.wait_ge(v_psum, 2 * (t // 2) + 2)
                nc.vector.tensor_tensor(v_all[:, :, t, :, :],
                                        ps[:, t // 2, (t % 2) * H:(t % 2) * H + H].rearrange("p (g j d) -> p g j d", g=NG, j=GH),
                                        v_bias.rearrange("p (g j d) -> p g j d", g=NG, j=GH), ALU.add).then_inc(v_ready, 1)

            steps = 0

            def route(ins):
                nonlocal steps
                steps += 1
                ins.then_inc(route_step, 1)
                dve.wait_ge(route_step, steps)

            dve.wait_ge(lg_psum, NT)
            route(nc.vector.tensor_copy(lg, ps[:, 6, 0:NT * E].rearrange("p (t e) -> p t e", t=NT)))
            nc.vector.tensor_reduce(top, lg, AX.X, ALU.max).then_inc(top_ready, 1)
            dve.wait_ge(top_ready, 1)
            route(nc.vector.tensor_tensor(pick, lg, top.unsqueeze(2).to_broadcast([P, NT, E]), ALU.is_equal))
            route(nc.vector.tensor_tensor(pick2, pick, weight_of, ALU.mult))
            route(nc.vector.tensor_reduce(pickmax, pick2, AX.X, ALU.max))
            route(nc.vector.tensor_tensor(onehot, pick2, pickmax.unsqueeze(2).to_broadcast([P, NT, E]), ALU.is_equal))
            nc.vector.tensor_copy(onehot_bf, onehot.rearrange("p t e -> p (t e)")).then_inc(onehot_ready, 1)
            dve.wait_ge(esc_ready, 1)
            route(nc.vector.tensor_scalar(esc1[:, :], esc[:, :], 1.0, None, ALU.add))
            nc.vector.reciprocal(score[:, :], esc1[:, :]).then_inc(score_ready, 1)
            dve.wait_ge(rank_psum, 1)
            nc.vector.tensor_copy(ranks.rearrange("p a t e -> p (a t e)"), ps[:, 7, 0:2 * NT * E]).then_inc(ranks_ready, 1)
            route(nc.vector.memset(passed[:, 0, :], 0.0))
            dve.wait_ge(ranks_ready, 1)
            for t in range(NT):
                route(nc.vector.tensor_tensor(passed[:, t + 1, :], passed[:, t, :], ranks[:, 1, t, :], ALU.add))
            route(nc.vector.tensor_tensor(cmp3, passed[:, NT, :].unsqueeze(2).to_broadcast([P, E, E]), steps_128, ALU.is_gt))
            route(nc.vector.tensor_reduce(tiles_of, cmp3, AX.X, ALU.add))
            route(nc.vector.tensor_tensor(cmp3, tiles_of.unsqueeze(1).to_broadcast([P, E, E]), earlier, ALU.mult))
            route(nc.vector.tensor_reduce(start_of, cmp3, AX.X, ALU.add))
            route(nc.vector.tensor_tensor(end_of, start_of, tiles_of, ALU.add))
            route(nc.vector.tensor_tensor(cmpj, end_of.unsqueeze(1).to_broadcast([P, TILES, E]), tile_no, ALU.is_le))
            route(nc.vector.tensor_reduce(tile_exp, cmpj, AX.X, ALU.add))
            route(nc.vector.tensor_scalar(tile_exp_i[:, :], tile_exp, float(E - 1), None, ALU.min))
            route(nc.vector.tensor_tensor(pick, passed[:, 0:NT, :], ranks[:, 0, :, :], ALU.add))
            route(nc.vector.scalar_tensor_tensor(pick2, start_of.unsqueeze(1).to_broadcast([P, NT, E]), float(P),
                                                 pick, ALU.mult, ALU.add))
            route(nc.vector.tensor_tensor(pick, pick2, onehot, ALU.mult))
            route(nc.vector.tensor_reduce(dest, pick, AX.X, ALU.add))
            nc.vector.tensor_copy(dest_i[:, :], dest).then_inc(dest_ready, 1)

            def row_max(n, c, i):
                dve.wait_ge(max_scores, n + 1)
                nc.vector.tensor_reduce(negmax[:, c, i:i + 1], ps[:, 2 + 2 * (i % 2):4 + 2 * (i % 2), :], AX.XY,
                                        ALU.max, negate=True).then_inc(max_read, 1)

            def negmax_cut(m, c):
                src = negmax[:, c, :]
                dve.wait_ge(max_read, 16 * (m + 1))
                if not isinstance(m, int) or m > 0:
                    dve.wait_ge(negmax_turned, m)
                nc.vector.tensor_copy(negmax_parts[:, 0:16], src).then_inc(split_step, 1)
                dve.wait_ge(split_step, 4 * m + 1)
                nc.vector.tensor_tensor(split1[:, :], src, negmax_parts[:, 0:16], ALU.subtract).then_inc(split_step, 1)
                dve.wait_ge(split_step, 4 * m + 2)
                nc.vector.tensor_copy(negmax_parts[:, 16:32], split1[:, :]).then_inc(split_step, 1)
                dve.wait_ge(split_step, 4 * m + 3)
                nc.vector.tensor_tensor(split2[:, :], split1[:, :], negmax_parts[:, 16:32], ALU.subtract).then_inc(split_step, 1)
                dve.wait_ge(split_step, 4 * m + 4)
                nc.vector.tensor_copy(negmax_parts[:, 32:48], split2[:, :]).then_inc(negmax_split, 1)

            for i in range(16):
                row_max(i, 0, i)
            negmax_cut(0, 0)
            for i in range(16):
                row_max(16 + i, 1, i)

            def half(g, c, maxima, negmax_next):
                m = 2 * g + c
                if negmax_next:
                    negmax_cut(m + 1, 1 - c)
                if maxima:
                    for i in range(16):
                        row_max(16 * (m + 2) + i, c, i)
                dve.wait_ge(acc_read, m + 3)
                nc.vector.memset(wait_slot[:, :], 0.0)
                nc.vector.stream_shuffle(rden[:, c, :], acc_sb[:, c, :], [HD] * STRIP).then_inc(den_ready, 1)
                dve.wait_ge(den_ready, m + 1)
                nc.vector.reciprocal(rden[:, c, :], rden[:, c, :]).then_inc(rden_ready, 1)

            with dve.Fori(0, NG - 1) as g:
                half(g, 0, True, True)
                half(g, 1, True, True)
            half(NG - 1, 0, False, True)
            half(NG - 1, 1, False, False)

            for t in range(NT):
                dve.wait_ge(token_psum, t + 1)
                nc.vector.tensor_tensor(resid[:, t, :], ps[:, 6 + t % 2, 0:H], resid[:, t, :], ALU.add).then_inc(token_summed, 1)

            def xt_copy(i):
                dve.wait_ge(tile_turned, i + 1)
                nc.vector.tensor_copy(tile_xt, ps[:, 2, 0:H].rearrange("p (k t) -> p k t", k=KH)).then_inc(tile_xt_ready, 1)

            def gate_up_product(i):
                dve.wait_ge(tile_gate_ready, i + 1)
                nc.vector.tensor_tensor(tile_h, ps[:, 1, :], tile_gate, ALU.mult).then_inc(tile_h_ready, 1)

            xt_copy(0)
            with dve.Fori(0, TILES - 1) as i:
                dve.wait_ge(tile_gu_psum, i + 1)
                xt_copy(i + 1)
                gate_up_product(i)
            gate_up_product(TILES - 1)
            for t in range(NT):
                dve.wait_ge(gathered_in, 16 * NT)
                dve.wait_ge(token_summed, NT)
                nc.vector.tensor_tensor(resid[:, t, :], resid[:, t, :], gathered[:, t, :], ALU.add).then_inc(final_ready, 1)

        @block.gpsimd
        def _(pool):
            nc.gpsimd.memset(minus_half[:, :], -0.5).then_inc(half_set, 1)
            nc.gpsimd.memset(probs_w[:, 0:H], 0.0).then_inc(zero_set, 1)
            nc.gpsimd.memset(ones_bf[:, :], 1.0).then_inc(ones_ready, 1)
            pool.wait_ge(half_set, 1)
            for hf in range(2):
                pool.wait_ge(veps_ready, hf + 1)
                nc.gpsimd.tensor_tensor(rstd[:, 4 * hf:4 * hf + 4], veps[:, 4 * hf:4 * hf + 4],
                                        minus_half[:, 4 * hf:4 * hf + 4], ALU.pow).then_inc(rstd_ready, 1)
            nc.gpsimd.memset(v_group[:, :, :, :], 1.0).then_inc(ones_ready, 1)
            pool.wait_ge(zero_set, 1)
            pool.dma_start(sorted_x.rearrange("(i p) d -> p i d", p=P),
                           probs_w[:, 0:H].unsqueeze(1).to_broadcast([P, TILES, H])).then_inc(zeros_in, 16)
            pool.wait_ge(vw_in, 48)
            for t in range(NT):
                pool.wait_ge(xn_ready, t + 1)
                nc.gpsimd.tensor_tensor(resid[:, t, :], resid[:, t, :], out_bias, ALU.add).then_inc(bias_added, 1)
            pool.wait_ge(v_ready, NT)
            pool.wait_ge(ones_ready, 2)
            for kt in range(NT):
                nc.gpsimd.tensor_copy(v_group[:, kt, :, 0:HD], v_all[:, 0, kt, :, :]).then_inc(vg_ready, 1)
            pool.wait_ge(score_ready, 1)
            pool.wait_ge(xt_psum, 4)
            for t in range(NT):
                nc.gpsimd.tensor_scalar(xn[:, t, :], xn[:, t, :], score[:, t:t + 1], None, ALU.mult).then_inc(scaled_ready, 1)
            pool.wait_ge(zeros_in, 16)
            for u in range(8):
                fc, c = u % 4, u // 4
                pool.wait_ge(gu_read, 2 * u + 2)
                nc.gpsimd.tensor_tensor(hid[:, fc, c * HALF:(c + 1) * HALF], sh_gate[u % 2], sh_up[u % 2], ALU.mult)\
                    .then_inc(hid_ready, 1)
            pool.wait_ge(dest_ready, 1)
            pool.wait_ge(scaled_ready, NT)
            for t in range(NT):
                pool.indirect_dma_start(out=sorted_x[:, :], out_offset=bass.IndirectOffsetOnAxis(ap=dest_i[:, t:t + 1], axis=0),
                                        in_=xn[:, t, :], in_offset=None).then_inc(scattered, 16)
            for i in range(2):
                nc.gpsimd.memset(token_pool[:, i:i + 1], 0.0).then_inc(attn_ready, 1)

            def half(g, c, refill):
                m = 2 * g + c
                if refill:
                    for kt in range(NT):
                        pool.wait_ge(probs_used, 2 + NT * m + kt + 1)
                        nc.gpsimd.tensor_copy(v_group[:, kt, :, 0:HD], v_all[:, bass.ds(g + 1, 1), kt, :, :].rearrange("p o j d -> p (o j) d"))\
                            .then_inc(vg_ready, 1)
                pool.wait_ge(rden_ready, m + 1)
                nc.gpsimd.tensor_tensor(attn[:, bass.ds(g, 1), c * HALF:(c + 1) * HALF].rearrange("p o t -> p (o t)"),
                                        acc_sb[:, c, :], rden[:, c, :], ALU.mult).then_inc(attn_ready, 1)

            with pool.Fori(0, NG - 1) as g:
                half(g, 0, False)
                half(g, 1, True)
            half(NG - 1, 0, False)
            half(NG - 1, 1, False)

            pool.wait_ge(tile_out, 16 * TILES)
            pool.wait_ge(token_psum, NT)
            for t in range(NT):
                pool.indirect_dma_start(out=gathered[:, t, :], out_offset=None, in_=sorted_y[:, :],
                                        in_offset=bass.IndirectOffsetOnAxis(ap=dest_i[:, t:t + 1], axis=0)).then_inc(gathered_in, 16)

        @block.tensor
        def _(pe):
            pe.wait_ge(consts_in, 16)
            for hf in range(2):
                pe.wait_ge(xn_ready, 4 * hf + 4)
                for k in range(KH):
                    for t in range(4):
                        last = pe.transpose(ps[:, 2 * hf + k, t * P:(t + 1) * P], xn[:, 4 * hf + t, k::KH], ident)
                    last.then_inc(xt_psum, 1)
            pe.wait_ge(latw_in, 32)
            for c in range(2):
                pe.wait_ge(xt_ready_a, c + 1)
                pe.wait_ge(xt_ready_v, c + 1)
                for k in range(KH):
                    last = pe.matmul(ps[:, 4 + c, :], lat_wt[:, k, :], x_t[:, k, c * HALF:(c + 1) * HALF],
                                     start=(k == 0), stop=(k == KH - 1))
                last.then_inc(lat_psum, 1)
            pe.wait_ge(upw_in, 48)
            for i in range(4):
                s, c = i % 2, i // 2
                pe.wait_ge(lat_ready, c + 1 if c == 0 else 2)
                rows = slice(64 * s, 64 * s + 64)
                for w in range(2):
                    last = pe.matmul(ps[:, 4 * c + 2 * s + w, :], up_wt[rows, w * P:(w + 1) * P],
                                     lat[rows, c * HALF:(c + 1) * HALF], start=True, stop=True)
                last.then_inc(up_psum, 1)
            pe.wait_ge(vw_in, 48)
            pe.wait_ge(up_read, 2)
            for t in range(NT):
                pe.matmul(ps[:, t // 2, (t % 2) * H:(t % 2) * H + H], lat[64:P, t * P:(t + 1) * P], v_wt[64:P, :],
                          start=True, stop=True).then_inc(v_psum, 1)
            pe.wait_ge(router_in, 16)
            pe.wait_ge(up_read, 4)
            for c in range(2):
                for k in range(KH):
                    last = pe.matmul(ps[0:E, 4 + c, :], router_t[:, k, :], x_t[:, k, c * HALF:(c + 1) * HALF],
                                     start=(k == 0), stop=(k == KH - 1))
                last.then_inc(lgt_psum, 1)
            pe.wait_ge(lgt_ready, 2)
            for t in range(NT):
                pe.transpose(ps[:, 6, t * E:(t + 1) * E], logit_t[0:E, t * P:(t + 1) * P], ident[0:E, 0:E]).then_inc(lg_psum, 1)
            pe.wait_ge(onehot_ready, 1)
            pe.wait_ge(casts_ready, 3)
            pe.wait_ge(ones_ready, 2)
            pe.matmul(ps[:, 7, 0:NT * E], before_bf[:, :], onehot_bf, start=True, stop=True)
            pe.matmul(ps[:, 7, NT * E:2 * NT * E], ones_bf[:, :], onehot_bf, start=True, stop=True).then_inc(rank_psum, 1)

            def max_tile(n, g, c, i):
                j, qt = i // 4, i % 4
                pe.wait_ge(max_read, n - 1)
                for kh in range(2):
                    last = pe.matmul(ps[:, 2 + 2 * (i % 2) + kh, :],
                                     q_stack[0:KROWS, c, bass.ds(GH * g + j, 1), qt * P:(qt + 1) * P].rearrange("p o t -> p (o t)"),
                                     k_stack[0:KROWS, bass.ds(GH * g + j, 1), kh * HALF:(kh + 1) * HALF].rearrange("p o t -> p (o t)"),
                                     start=True, stop=True)
                last.then_inc(max_scores, 1)

            def negmax_turn(m, c):
                pe.wait_ge(negmax_split, m + 1)
                pe.transpose(ps[:, 6 + c, 0:64].bitcast(BF16), negmax_parts[:, :], ident_bf[:, :]).then_inc(negmax_turned, 1)

            pe.wait_ge(ranks_ready, 1)
            pe.wait_ge(v_ready, NT)
            pe.wait_ge(lgt_ready, 2)
            pe.wait_ge(stacks_in[0], 16 * 18)
            pe.wait_ge(sgu_in, 16)
            for u in range(8):
                fc, c = u % 4, u // 4
                b = 0 if u % 2 == 0 else 6
                if u >= 2:
                    pe.wait_ge(gu_read, 2 * (u - 1))
                for w in range(2):
                    for k in range(KH):
                        last = pe.matmul(ps[:, b + w, :], sgu[:, k, w * F + fc:(w + 1) * F:KF],
                                         x_t[:, k, c * HALF:(c + 1) * HALF], start=(k == 0), stop=(k == KH - 1))
                        if u == 7 and k == 0:
                            last.then_inc(probs_used, 1)
                last.then_inc(gu_psum, 1)
                for i in range(4 * u, 4 * u + 4):
                    if i >= 2:
                        max_tile(i, 0, i // 16, i % 16)
                    else:
                        for kh in range(2):
                            last = pe.matmul(ps[:, 2 + 2 * (i % 2) + kh, :], q_stack[0:KROWS, 0, 0, i * P:(i + 1) * P],
                                             k_stack[0:KROWS, 0, kh * HALF:(kh + 1) * HALF], start=True, stop=True)
                        last.then_inc(max_scores, 1)
            pe.wait_ge(gu_read, 16)
            negmax_turn(0, 0)
            pe.wait_ge(stacks_in[1], 16 * 18)
            pe.wait_ge(stacks_in[2], 16 * 36)

            def half(g, c, maxima, negmax_next):
                m = 2 * g + c

                def score_tile(kt, j):
                    n = GH * (NT * m + kt) + j
                    pe.wait_ge(probs_ready, n + 1)
                    pe.matmul(ps[:, j % 2, :],
                              k_stack[0:ROWS, bass.ds(GH * g + j, 1), kt * P:(kt + 1) * P].rearrange("p o t -> p (o t)"),
                              q_stack[0:ROWS, c, bass.ds(GH * g + j, 1), :].rearrange("p o t -> p (o t)"),
                              start=True, stop=True).then_inc(scores_psum, 1)

                def weigh(kt):
                    step = NT * m + kt
                    pe.wait_ge(probs_ready, GH * step + GH + 2)
                    if c == 0:
                        pe.wait_ge(vg_ready, NT * g + kt + 1)
                    for j in range(GH):
                        last = pe.matmul(ps[STRIP * j:STRIP * j + STRIP, 6 + c, :], v_group[:, kt, j, :], probs[:, kt % 2, j, :],
                                         start=(kt == 0), stop=(kt == NT - 1))
                    last.then_inc(probs_used, 1)

                pe.wait_ge(negmax_in, 48 * (m + 1))
                for kt in range(NT):
                    score_tile(kt, 0)
                    score_tile(kt, 1)
                    if kt == 1:
                        pe.wait_ge(acc_read, m + 1)
                        pe.wait_ge(negmax_copied, m + 1)
                    if kt >= 1:
                        weigh(kt - 1)
                    score_tile(kt, 2)
                    score_tile(kt, 3)
                    if kt == 2 and negmax_next:
                        pe.wait_ge(acc_read, m + 2)
                        negmax_turn(m + 1, 1 - c)
                    if maxima:
                        for i in (2 * kt, 2 * kt + 1):
                            max_tile(16 * (m + 2) + i, g + 1, c, i)
                weigh(NT - 1)

            with pe.Fori(0, NG - 1) as g:
                half(g, 0, True, True)
                half(g, 1, True, True)
            half(NG - 1, 0, False, True)
            half(NG - 1, 1, False, False)

            pe.wait_ge(tail_in, 32)
            pe.wait_ge(hid_ready, 8)
            pe.wait_ge(attn_ready, 2 + 2 * NG)
            pe.wait_ge(acc_read, 2 + 2 * NG)
            for t in range(NT):
                if t >= 2:
                    pe.wait_ge(token_summed, t - 1)
                tt = slice(t * P, (t + 1) * P)
                for k in range(KF):
                    pe.matmul(ps[:, 6 + t % 2, 0:H], hid[:, k, tt], sdn[:, k, :], start=(k == 0), stop=False)
                for g in range(NG):
                    last = pe.matmul(ps[:, 6 + t % 2, 0:H], attn[:, g, tt], wout[:, g, :], start=False, stop=(g == NG - 1))
                last.then_inc(token_psum, 1)

            def turn_tile(i):
                pe.wait_ge(tile_in, 16 * (i + 1))
                for k in range(KH):
                    last = pe.transpose(ps[:, 2, k * P:(k + 1) * P], tile_x[:, k::KH], ident)
                last.then_inc(tile_turned, 1)

            def expert_of(i):
                return pe.value_load(tile_exp_i[0:1, bass.ds(i, 1)], min_val=0, max_val=E - 1)

            def weights(e, at_, n):
                return exp_w[:, bass.ds(e, 1), at_:at_ + n].rearrange("p o n -> p (o n)")

            def gate_up_tile(i, e):
                pe.wait_ge(tile_xt_ready, i + 1)
                for w in range(2):
                    for k in range(KH):
                        last = pe.matmul(ps[:, w, :], tile_xt[:, k, :], weights(e, k * GU + w * F, F),
                                         start=(k == 0), stop=(k == KH - 1))
                last.then_inc(tile_gu_psum, 1)

            def turn_h(i):
                pe.wait_ge(tile_h_ready, i + 1)
                for k in range(KF):
                    last = pe.transpose(ps[:, 3, k * P:(k + 1) * P], tile_h[:, k::KF], ident)
                last.then_inc(tile_ht_psum, 1)

            def down_tile(i, e):
                pe.wait_ge(tile_ht_ready, i + 1)
                for k in range(KF):
                    last = pe.matmul(ps[:, 5, 0:H], tile_ht[:, k, :], weights(e, KH * GU + k * H, H),
                                     start=(k == 0), stop=(k == KF - 1))
                last.then_inc(tile_y_psum, 1)

            pe.wait_ge(exp_low_in, 16 * E)
            pe.wait_ge(exp_high_in, 16 * E)
            turn_tile(0)
            gate_up_tile(0, expert_of(0))
            turn_tile(1)
            turn_h(0)
            with pe.Fori(1, TILES - 1) as i:
                gate_up_tile(i, expert_of(i))
                turn_tile(i + 1)
                down_tile(i - 1, expert_of(i - 1))
                turn_h(i)
            gate_up_tile(TILES - 1, expert_of(TILES - 1))
            pe.wait_ge(tile_y_ready, TILES - 2)
            down_tile(TILES - 2, expert_of(TILES - 2))
            turn_h(TILES - 1)
            pe.wait_ge(tile_y_ready, TILES - 1)
            down_tile(TILES - 1, expert_of(TILES - 1))


def _constants():
    ident = np.eye(P, dtype=np.float32)
    before = np.triu(np.ones((P, P), np.float32), 1)
    weight_of = np.tile(np.arange(E, 0, -1, dtype=np.float32), NT)
    steps_128 = np.tile(P * np.arange(E, dtype=np.float32), E)
    earlier = np.tril(np.ones((E, E), np.float32), -1).reshape(-1)
    tile_no = np.repeat(np.arange(TILES, dtype=np.float32), E)
    row = np.concatenate([weight_of, steps_128, earlier, tile_no])
    return np.concatenate([ident, before, np.tile(row, (P, 1))], 1)


def _rope():
    dim = H // 4
    inv = (np.float32(1) / np.float32(10000.0) ** (np.arange(0, dim, 2, dtype=np.float32) / np.float32(dim))).astype(np.float32)
    freq = np.outer(np.arange(T, dtype=np.float32), inv).astype(np.float32).T
    cos, sin = np.cos(freq).astype(np.float32), np.sin(freq).astype(np.float32)
    return np.concatenate([cos] * 4), np.concatenate([-sin, -sin, sin, sin])


def kernel(**inputs):
    import concourse.bacc as bacc
    from concourse.bass_utils import run_bass_kernel_spmd

    a = {k.split("_", 1)[1]: np.asarray(v) for k, v in inputs.items()}
    swap = np.r_[64:128, 0:64]
    wq, wk = a["attn_Wq_up"].T, a["attn_Wk_up"].T
    bq, bk = a["attn_bq_up"], a["attn_bk_up"]
    wo = a["attn_Wo"].T.reshape(NG, GH, HD, H)
    wo_pad = np.zeros((GH, STRIP, NG, H), np.float32)
    wo_pad[:, :HD] = wo.transpose(1, 2, 0, 3)
    v_w = np.zeros((P, H), np.float32)
    v_w[64:] = a["attn_Wv_up"].T
    cos, sin = _rope()
    arrays = {
        "x": a["attn_hidden_states"].reshape(T, H),
        "lat_w": np.concatenate([a["attn_Wq_down"].T, a["attn_Wkv_down"].T], 1),
        "lat_b": np.concatenate([a["attn_bq_down"], a["attn_bkv_down"]])[:, None],
        "up_w": np.concatenate([np.concatenate([wq, wq[:, swap]], 1), np.concatenate([wk, wk[:, swap]], 1)], 0),
        "up_b": np.stack([bq, bq[swap], bk, bk[swap]], 1),
        "v_w": v_w,
        "v_b": a["attn_bv_up"],
        "rope_c": cos,
        "rope_s": sin,
        "router_w": a["ffn_router_w"].T,
        "sgu_w": np.concatenate([a["ffn_shared_gate_w"], a["ffn_shared_up_w"]], 1),
        "sdn_w": a["ffn_shared_down_w"],
        "out_w": wo_pad.reshape(P, NG, H),
        "out_b": a["attn_bo"],
        "gate_up": a["ffn_gate_up_proj"],
        "down": a["ffn_down_proj"],
        "consts": _constants(),
        "one_rows": np.ones((ROWS - KROWS, NH, T), mybir.dt.np(BF16)),
    }
    nc = bacc.Bacc("TRN2", target_bir_lowering=False, num_devices=1)
    args = []
    for name, value in arrays.items():
        arrays[name] = np.ascontiguousarray(value)
        args.append(nc.dram_tensor(name, arrays[name].shape, mybir.dt.from_np(arrays[name].dtype), kind="ExternalInput").ap())
    out = nc.dram_tensor("out", [T, H], F32, kind="ExternalOutput").ap()
    build_kernel(nc, *args, out)
    result = run_bass_kernel_spmd(nc, [arrays], core_ids=[0])
    return result.results[0]["out"].reshape(1, T, H)
```

```python
from contextlib import ExitStack

import numpy as np

import concourse.bass as bass
from concourse import mybir

F32 = mybir.dt.float32
BF16 = mybir.dt.bfloat16
I32 = mybir.dt.int32
ALU = mybir.AluOpType
ACT = mybir.ActivationFunctionType
AX = mybir.AxisListType

P = 128
T, H = 1024, 256
NH, HD, LAT = 16, 16, 64
E, F = 8, 512
EPS = 1e-5
NT = T // P
KH, KF = H // P, F // P
GH = 4
NG = NH // GH
HALF = T // 2
STRIP = P // GH
PARTS_Q = (0, 0, 0, 1, 1, 2)
PARTS_K = (0, 1, 2, 0, 1, 0)
KROWS = len(PARTS_Q) * HD
ROWS = KROWS + 3
TILES = T // P + E - 1
EARLY = 4
GU = 2 * F
WEXP = KH * GU + KF * H

STACK = GH * T
STACKS_AT = (E // 2) * WEXP
ARENA = STACKS_AT + NG * STACK
STACK_LOADS = 18
LEAD = 3
AHEAD = 24
UP = ((1, 0), (0, 0), (1, 1), (0, 1))


def build_kernel(nc, x, lat_w, lat_b, up_w, up_b, v_w, v_b, rope_c, rope_s, router_w, sgu_w, sdn_w,
                 out_w, out_b, gate_up, down, consts, one_rows, out):
    nc.disable_value_cache = True
    ctx = ExitStack()
    with ctx:
        def sb(name, shape, dt=F32):
            return ctx.enter_context(nc.sbuf_tensor(name, shape, dt))

        def sem(name):
            return ctx.enter_context(nc.semaphore(name))

        ps = ctx.enter_context(nc.psum_tensor("ps", [P, 8, 512], F32))

        part_dram = [nc.dram_tensor(f"parts_{s}", [3, 2, P, T], BF16, kind="Internal").ap() for s in "qk"]
        sorted_x = nc.dram_tensor("sorted_x", [TILES * P, H], F32, kind="Internal").ap()
        sorted_y = nc.dram_tensor("sorted_y", [TILES * P, H], F32, kind="Internal").ap()

        arena = sb("arena", [P, ARENA])
        resid = sb("resid", [P, NT, H])
        v_ones = sb("v_ones", [P, NG, NT, GH, STRIP])
        probs = sb("probs", [P, 2, GH, HALF])
        work = sb("work", [P, 6 * T])
        hid = sb("hid", [P, KF, T])
        den = sb("den", [P, HALF])
        rden = sb("rden", [P, HALF])
        cst = sb("cst", [P, 2 * P + 3 * 64 + TILES * E + 3])
        ident_bf = sb("ident_bf", [P, P], BF16)
        before_bf = sb("before_bf", [P, P], BF16)
        ones_bf = sb("ones_bf", [P, P], BF16)
        lat_bias = sb("lat_bias", [P, 1])
        up_bias = sb("up_bias", [P, 4])
        stats = sb("stats", [P, NT, 6])
        mv = sb("mv", [P, NT, 2])
        veps = sb("veps", [P, NT])
        minus_half = sb("minus_half", [P, NT])
        rstd = sb("rstd", [P, NT])
        token_pool = sb("token_pool", [P, 2])
        wait_slot = sb("wait_slot", [P, 1])
        token_act = sb("token_act", [P, 4])
        negmax = sb("negmax", [P, 2, GH * 4])
        split1 = sb("split1", [P, GH * 4])
        split2 = sb("split2", [P, GH * 4])
        negmax_parts = sb("negmax_parts", [P, P], BF16)
        negmax_rows = sb("negmax_rows", [3 * GH * 4, P], BF16)
        tile_exp_i = sb("tile_exp_i", [P, TILES], I32)
        dest_i = sb("dest_i", [P, NT], I32)
        esc = sb("esc", [P, NT])
        esc1 = sb("esc1", [P, NT])
        score = sb("score", [P, NT])

        def words(at, n):
            return arena[:, at:at + n]

        stacks = words(STACKS_AT, NG * STACK).bitcast(BF16).rearrange("p (g n) -> p g n", g=NG)
        q_stack = stacks[:, :, 0:STACK].rearrange("p g (c h t) -> p g c h t", c=2, h=GH)
        k_stack = stacks[:, :, STACK:2 * STACK].rearrange("p g (h t) -> p g h t", h=GH)
        exp_w = words(0, E * WEXP).rearrange("p (e n) -> p e n", e=E)
        at = 0

        def temp(n):
            nonlocal at
            at += n
            return words(at - n, n)

        cos_t, sin_t = temp(T), temp(T)
        plain = temp(2 * T).rearrange("p (s t) -> p s t", s=2)
        parts = temp(2 * 3 * T // 2).bitcast(BF16).rearrange("p (s a t) -> p s a t", s=2, a=3)
        lat = temp(T)
        logit_t = lat
        lat_wt = temp(KH * P).rearrange("p (k n) -> p k n", k=KH)
        up_wt = temp(4 * P)
        v_wt = temp(H)
        v_bias = temp(H)
        out_bias = temp(H)
        router_t = temp(KH * E).rearrange("p (k e) -> p k e", k=KH)
        te = "p (t e) -> p t e"
        lg, pick, pick2, onehot = [temp(NT * E).rearrange(te, t=NT) for _ in range(4)]
        top, pickmax, dest = temp(NT), temp(NT), temp(NT)
        onehot_bf = temp(NT * E // 2).bitcast(BF16)
        ranks = temp(2 * NT * E).rearrange("p (a t e) -> p a t e", a=2, t=NT)
        passed = temp((NT + 1) * E).rearrange(te, e=E)
        cmp3 = temp(E * E).rearrange("p (e m) -> p e m", e=E)
        tiles_of, start_of, end_of = temp(E), temp(E), temp(E)
        cmpj = temp(TILES * E).rearrange(te, e=E)
        tile_exp = temp(TILES)
        assert at <= STACKS_AT, at

        v_words = v_ones[:, 0:2, :, :, :].rearrange("p g t j d -> p (g t j d)")
        sdn = v_words[:, 0:KF * H].rearrange("p (k n) -> p k n", k=KF)
        wout = v_words[:, KF * H:KF * H + 2 * H].rearrange("p (g n) -> p g n", g=2)

        attn = work[:, 4 * T:6 * T].rearrange("p (r t) -> p r t", r=2)
        x_t = work[:, 4 * T:6 * T].rearrange("p (k t) -> p k t", k=KH)
        sgu = work[:, 2 * T:4 * T].rearrange("p (k n) -> p k n", k=KH)
        xn = work[:, 0:2 * T].rearrange("p (t d) -> p t d", t=NT)
        acc_sb = work[:, 0:4 * T].rearrange("p (r c w n) -> p r c w n", r=2, c=2, w=2)
        gathered = xn
        probs_w = probs[:, :, :, :].rearrange("p a j t -> p (a j t)")
        sh_gate = [probs_w[:, 1024 * u:1024 * u + 512] for u in range(2)]
        sh_up = [probs_w[:, 1024 * u + 512:1024 * u + 1024] for u in range(2)]
        rot_b = [probs_w[:, 2048 + 512 * n:2560 + 512 * n] for n in range(4)]
        res = words(STACKS_AT + (NG - 1) * STACK, 4 * HALF).rearrange("p (u n) -> p u n", u=4)
        res1 = [res[:, u, :] for u in range(2)]
        res2 = [res[:, 2 + u, :] for u in range(2)]
        tile_x = probs_w[:, 0:256]
        tile_xt = probs_w[:, 256:512].rearrange("p (k t) -> p k t", k=KH)
        tile_gate = probs_w[:, 512:1024]
        tile_h = probs_w[:, 1024:1536]
        tile_ht = probs_w[:, 1536:2048].rearrange("p (k t) -> p k t", k=KF)
        tile_y = probs_w[:, 2048:2304]

        ident = cst[:, 0:P]
        before = cst[:, P:2 * P]
        c0 = 2 * P
        weight_of = cst[:, c0:c0 + 64].rearrange("p (t e) -> p t e", t=NT)
        steps_128 = cst[:, c0 + 64:c0 + 128].rearrange("p (e m) -> p e m", e=E)
        earlier = cst[:, c0 + 128:c0 + 192].rearrange("p (e m) -> p e m", e=E)
        tile_no = cst[:, c0 + 192:c0 + 192 + TILES * E].rearrange("p (j e) -> p j e", j=TILES)
        rows_of = cst[:, c0 + 192 + TILES * E:]

        x_in = [sem(f"x_in{i}") for i in range(4)]
        consts_in, latw_in, upw_in, rope_in = sem("consts_in"), sem("latw_in"), sem("upw_in"), sem("rope_in")
        vw_in, router_in, sgu_in, tail_in = sem("vw_in"), sem("router_in"), sem("sgu_in"), sem("tail_in")
        stats_ready, mv_ready, veps_ready = sem("stats_ready"), sem("mv_ready"), sem("veps_ready")
        rstd_ready, half_set = sem("rstd_ready"), sem("half_set")
        xn_ready, xt_psum, xt_ready_a, xt_ready_v = sem("xn_ready"), sem("xt_psum"), sem("xt_ready_a"), sem("xt_ready_v")
        casts_ready, ones_ready = sem("casts_ready"), sem("ones_ready")
        lat_psum, lat_ready = sem("lat_psum"), sem("lat_ready")
        up_psum, plain_ready, swap_psum, swap_read = sem("up_psum"), sem("plain_ready"), sem("swap_psum"), sem("swap_read")
        rot_a_ready, rot_ready = sem("rot_a_ready"), sem("rot_ready")
        high_ready, res1_ready, mid_ready = sem("high_ready"), sem("res1_ready"), sem("mid_ready")
        res2_ready, low_ready = sem("res2_ready"), sem("low_ready")
        parts_stored = [sem(f"parts_stored_{i}") for i in range(8)]
        stacks_in = [sem(f"stacks_in{i}") for i in range(NG)]
        v_psum, v_ready = sem("v_psum"), sem("v_ready")
        lgt_psum, lgt_ready, lg_psum, lg_ready = sem("lgt_psum"), sem("lgt_ready"), sem("lg_psum"), sem("lg_ready")
        route_step, onehot_ready, rank_psum, ranks_ready = sem("route_step"), sem("onehot_ready"), sem("rank_psum"), sem("ranks_ready")
        top_ready, esc_ready, score_ready, dest_ready = sem("top_ready"), sem("esc_ready"), sem("score_ready"), sem("dest_ready")
        scaled_ready, zero_set, zeros_in, scattered = sem("scaled_ready"), sem("zero_set"), sem("zeros_in"), sem("scattered")
        bias_added = sem("bias_added")
        gu_psum, gu_read, up_copied, hid_ready = sem("gu_psum"), sem("gu_read"), sem("up_copied"), sem("hid_ready")
        max_scores, max_read = sem("max_scores"), sem("max_read")
        split_step, negmax_split, negmax_turned = sem("split_step"), sem("negmax_split"), sem("negmax_turned")
        negmax_copied, negmax_in = sem("negmax_copied"), sem("negmax_in")
        scores_psum, probs_ready, probs_used = sem("scores_psum"), sem("probs_ready"), sem("probs_used")
        acc_read, den_ready, rden_ready, attn_ready = sem("acc_read"), sem("den_ready"), sem("rden_ready"), sem("attn_ready")
        num_ready, inverted = sem("num_ready"), sem("inverted")
        exp_low_in, exp_high_in = sem("exp_low_in"), sem("exp_high_in")
        token_psum, token_summed = sem("token_psum"), sem("token_summed")
        tile_in, tile_turned, tile_xt_ready = sem("tile_in"), sem("tile_turned"), sem("tile_xt_ready")
        tile_gu_psum, tile_gate_ready, tile_h_ready = sem("tile_gu_psum"), sem("tile_gate_ready"), sem("tile_h_ready")
        tile_ht_psum, tile_ht_ready, tile_y_psum = sem("tile_ht_psum"), sem("tile_ht_ready"), sem("tile_y_psum")
        tile_y_ready, tile_out = sem("tile_y_ready"), sem("tile_out")
        gathered_in = [sem(f"gathered_in{t}") for t in range(NT)]
        final_ready, stored = sem("final_ready"), sem("stored")

        x_dram = x.rearrange("(t p) d -> p t d", p=P)
        out_dram = out.rearrange("(t p) d -> p t d", p=P)

        def part_rows(s, a, b, g, c0, c1):
            rows = slice((g % 2) * GH * HD, (g % 2 + 1) * GH * HD)
            return part_dram[s][a:b, g // 2, rows, c0:c1].rearrange("a (h d) t -> a d h t", d=HD)

        block = ctx.enter_context(nc.Block())

        @block.sync
        def _(sp):
            sp.dma_start(resid[:, 0:2, :], x_dram[:, 0:2, :]).then_inc(x_in[0], 16)
            sp.dma_start(resid[:, 4:6, :], x_dram[:, 4:6, :]).then_inc(x_in[2], 16)
            sp.dma_start(cst[:, :], consts).then_inc(consts_in, 16)
            sp.dma_start(lat_wt, lat_w.rearrange("(p k) n -> p k n", k=KH)).then_inc(latw_in, 16)
            sp.dma_start(lat_bias[:, :], lat_b).then_inc(latw_in, 16)
            sp.dma_start(up_wt, up_w).then_inc(upw_in, 16)
            sp.dma_start(up_bias[:, :], up_b).then_inc(upw_in, 16)
            sp.dma_start(sgu, sgu_w.rearrange("(p k) n -> p k n", k=KH)).then_inc(sgu_in, 16)
            sp.dma_start(k_stack[KROWS:ROWS], one_rows.rearrange("r (g h) t -> r g h t", g=NG)).then_inc(upw_in, 16)
            sp.dma_start(router_t, router_w.rearrange("(p k) e -> p k e", k=KH)).then_inc(router_in, 16)

            def store_parts(n, half_):
                s, c = UP[n % 4]
                sp.wait_ge(low_ready, n + 1)
                sp.dma_start(part_dram[s][:, half_, :, c * HALF:(c + 1) * HALF].rearrange("a p t -> p a t"),
                             parts[:, s, :, c * HALF:(c + 1) * HALF]).then_inc(parts_stored[n], 16)

            def load_stacks(g):
                for row, n_parts in ((0, 3), (3, 2), (5, 1)):
                    for a in range(n_parts):
                        sp.dma_start(k_stack[HD * (row + a):HD * (row + a + 1), g, :, :],
                                     part_rows(1, a, a + 1, g, 0, T).rearrange("a d h t -> (a d) h t")).then_inc(stacks_in[g], 16)
                for row, a in enumerate(PARTS_Q):
                    for c in range(2):
                        sp.dma_start(q_stack[HD * row:HD * row + HD, g, c, :, :],
                                     part_rows(0, a, a + 1, g, c * HALF, (c + 1) * HALF).rearrange("a d h t -> (a d) h t"))\
                            .then_inc(stacks_in[g], 16)

            def negmax_load(m, g, c):
                sp.wait_ge(negmax_copied, m + 1)
                for a in range(3):
                    sp.dma_start(q_stack[KROWS + a:KROWS + a + 1, g, c, :, :].rearrange("p h t -> p (h t)"),
                                 negmax_rows[16 * a:16 * a + 16, :]).then_inc(negmax_in, 16)

            def load_expert(e, loaded):
                sp.dma_start(exp_w[:, e, 0:KH * GU], gate_up[e].rearrange("(p k) n -> p (k n)", k=KH)).then_inc(loaded, 16)
                sp.dma_start(exp_w[:, e, KH * GU:], down[e].rearrange("(p k) n -> p (k n)", k=KF)).then_inc(loaded, 16)

            for n in range(4):
                store_parts(n, 0)
            for n in range(4):
                sp.wait_ge(parts_stored[n], 16)
            load_stacks(0)
            load_stacks(1)
            for n in range(4, 8):
                if n == 7:
                    negmax_load(0, 0, 0)
                store_parts(n, 1)
            for n in range(4, 8):
                sp.wait_ge(parts_stored[n], 16)
            load_stacks(2)
            negmax_load(1, 0, 1)
            load_stacks(3)
            sp.wait_ge(v_ready, 2 * NT)
            sp.wait_ge(lg_psum, NT)
            sp.wait_ge(bias_added, NT)
            sp.wait_ge(dest_ready, 1)
            for e in range(E // 2):
                load_expert(e, exp_low_in)
            for g in range(1, NG):
                negmax_load(2 * g, g, 0)
                negmax_load(2 * g + 1, g, 1)
                sp.wait_ge(max_scores, 32 * g)
                sp.wait_ge(scores_psum, 2 * GH * NT * g)
                load_expert(E // 2 + g - 1, exp_high_in)
            load_expert(E - 1, exp_high_in)
            sp.wait_ge(probs_used, 2 + 4 * NT)
            sp.dma_start(sdn, sdn_w.rearrange("(p k) n -> p k n", k=KF)).then_inc(tail_in, 16)
            sp.dma_start(wout, out_w).then_inc(tail_in, 16)

            sp.wait_ge(scattered, 16 * NT)
            sp.wait_ge(probs_used, 2 + 8 * NT)
            sp.dma_start(tile_x, sorted_x[0:P, :]).then_inc(tile_in, 16)
            with sp.Fori(1, TILES) as i:
                sp.wait_ge(tile_turned, i)
                sp.dma_start(tile_x, sorted_x[bass.ds(i * P, P), :]).then_inc(tile_in, 16)

            for t in range(NT):
                sp.wait_ge(final_ready, t + 1)
                sp.dma_start(out_dram[:, t, :], resid[:, t, :]).then_inc(stored, 16)
            sp.wait_ge(stored, 16 * NT)

        @block.scalar
        def _(act):
            act.dma_start(resid[:, 2:4, :], x_dram[:, 2:4, :]).then_inc(x_in[1], 16)
            act.dma_start(resid[:, 6:8, :], x_dram[:, 6:8, :]).then_inc(x_in[3], 16)
            act.dma_start(cos_t, rope_c).then_inc(rope_in, 16)
            act.dma_start(sin_t, rope_s).then_inc(rope_in, 16)
            act.dma_start(v_wt, v_w).then_inc(vw_in, 16)
            act.dma_start(v_bias, v_b.partition_broadcast(P)).then_inc(vw_in, 16)
            act.dma_start(out_bias, out_b.partition_broadcast(P)).then_inc(vw_in, 16)

            for hf in range(2):
                act.wait_ge(xt_psum, 2 * hf + 1)
                nc.scalar.copy(x_t[:, 0, hf * HALF:(hf + 1) * HALF], ps[:, 2 * hf, :]).then_inc(xt_ready_a, 1)
            act.wait_ge(latw_in, 32)
            for c in range(2):
                act.wait_ge(lat_psum, c + 1)
                nc.scalar.activation(lat[:, c * HALF:(c + 1) * HALF], ps[:, 4 + c, :], ACT.Identity,
                                     bias=lat_bias[:, 0:1]).then_inc(lat_ready, 1)
            act.wait_ge(upw_in, 48)

            def piece(n, a, src):
                s, c = UP[n % 4]
                return nc.scalar.copy(parts[:, s, a, c * HALF:(c + 1) * HALF], src)

            def middle(n):
                act.wait_ge(res1_ready, n + 1)
                piece(n, 1, res1[n % 2]).then_inc(mid_ready, 1)

            def low(n):
                act.wait_ge(res2_ready, n + 1)
                act.wait_ge(mid_ready, n + 1)
                act.wait_ge(high_ready, n + 1)
                piece(n, 2, res2[n % 2]).then_inc(low_ready, 1)

            for n in range(6):
                if n < 4:
                    s, c = UP[n]
                    act.wait_ge(up_psum, n + 1)
                    nc.scalar.activation(plain[:, s, c * HALF:(c + 1) * HALF], ps[:, (6 + n) % 8, :], ACT.Identity,
                                         bias=up_bias[:, 2 * s:2 * s + 1]).then_inc(plain_ready, 1)
                    act.wait_ge(plain_ready, n + 1)
                    piece(n, 0, plain[:, s, c * HALF:(c + 1) * HALF]).then_inc(high_ready, 1)
                if 1 <= n < 5:
                    middle(n - 1)
                if n >= 2:
                    low(n - 2)
            for c in range(2):
                act.wait_ge(lgt_psum, c + 1)
                nc.scalar.copy(logit_t[0:E, c * HALF:(c + 1) * HALF], ps[0:E, 2 + c, :]).then_inc(lgt_ready, 1)
            act.wait_ge(top_ready, 1)
            nc.scalar.activation(esc[:, :], top, ACT.Exp, scale=-1.0).then_inc(esc_ready, 1)

            def shared_unit(u):
                b = 0 if u % 2 == 0 else 6
                act.wait_ge(gu_psum, u + 1)
                if u >= 2:
                    act.wait_ge(hid_ready, u - 1)
                nc.scalar.activation(sh_gate[u % 2], ps[:, b, :], ACT.Silu).then_inc(gu_read, 1)
                nc.scalar.copy(sh_up[u % 2], ps[:, b + 1, :]).then_inc(gu_read, 1)

            act.wait_ge(zeros_in, 16)
            for n in range(4):
                if n == 3:
                    act.wait_ge(negmax_turned, 1)
                    nc.scalar.copy(negmax_rows[:, :], ps[0:48, 6, 0:64].bitcast(BF16)).then_inc(negmax_copied, 1)
                shared_unit(2 * n)
                act.wait_ge(rot_ready, n + 1)
                act.wait_ge(parts_stored[n], 16)
                s, c = UP[n]
                piece(4 + n, 0, plain[:, s, c * HALF:(c + 1) * HALF]).then_inc(high_ready, 1)
                shared_unit(2 * n + 1)
                if n < 3:
                    middle(4 + n)
                    low(4 + n)

            def negmax_copy(m, c):
                act.wait_ge(negmax_turned, m + 1)
                act.wait_ge(negmax_in, 48 * m)
                nc.scalar.copy(negmax_rows[:, :], ps[0:48, 6 + c, 0:64].bitcast(BF16)).then_inc(negmax_copied, 1)

            for i, token in enumerate((probs_ready, probs_ready, acc_read, acc_read)):
                nc.scalar.copy(token_act[:, i:i + 1], esc[:, 0:1]).then_inc(token, 2 if i >= 2 else 1)

            def exps(g, c, kt):
                step = NT * (2 * g + c) + kt
                for j in range(GH):
                    act.wait_ge(scores_psum, GH * step + j + 1)
                    if j == 0:
                        act.wait_ge(probs_used, step + 1)
                    nc.scalar.activation(probs[:, kt % 2, j, :], ps[:, j % 2, :], ACT.Exp,
                                         scale=HD ** -0.5).then_inc(probs_ready, 1)

            def acc_copy(g, c):
                m = 2 * g + c
                act.wait_ge(probs_used, 2 + NT * (m + 1))
                act.wait_ge(scattered, 16 * NT)
                act.wait_ge(attn_ready, 2 * (g // 2) + c + 1)
                for w in range(2):
                    nc.scalar.activation(acc_sb[:, bass.ds(g % 2, 1), c, w, :].rearrange("p o t -> p (o t)"), ps[:, 6 + c, :],
                                         ACT.Copy, scale=rows_of[:, bass.ds(g % 2 + w, 1)]).then_inc(acc_read, 1)

            def half(g, c, last=False):
                for kt in range(LEAD, NT):
                    exps(g, c, kt)
                    if kt == 5 and not last:
                        negmax_copy(2 * g + c + 1, 1 - c)
                if last:
                    acc_copy(g, c)
                    return
                for kt in range(LEAD):
                    exps(g + c, 1 - c, kt)
                    if kt == 0:
                        acc_copy(g, c)

            middle(7)
            act.wait_ge(hid_ready, 8)
            for kt in range(LEAD):
                exps(0, 0, kt)
                if kt == 0:
                    low(7)
            with act.Fori(0, NG - 1) as g:
                half(g, 0)
                half(g, 1)
            half(NG - 1, 0)
            half(NG - 1, 1, last=True)

            def evacuate(i):
                act.wait_ge(tile_gu_psum, i + 1)
                nc.scalar.activation(tile_gate, ps[:, 0, :], ACT.Silu).then_inc(tile_gate_ready, 1)

            def down_out(i):
                act.wait_ge(tile_y_psum, i + 1)
                if not isinstance(i, int) or i > 0:
                    act.wait_ge(tile_out, 16 * i)
                nc.scalar.copy(tile_y, ps[:, 5, 0:H]).then_inc(tile_y_ready, 1)
                act.wait_ge(tile_y_ready, i + 1)
                act.dma_start(sorted_y[bass.ds(i * P, P), :], tile_y).then_inc(tile_out, 16)

            def ht_copy(i):
                act.wait_ge(tile_ht_psum, i + 1)
                nc.scalar.copy(tile_ht, ps[:, 3, :].rearrange("p (k t) -> p k t", k=KF)).then_inc(tile_ht_ready, 1)

            evacuate(0)
            ht_copy(0)
            evacuate(1)
            down_out(0)
            ht_copy(1)
            with act.Fori(2, TILES) as i:
                evacuate(i)
                down_out(i - 1)
                ht_copy(i)
            down_out(TILES - 1)

        @block.vector
        def _(dve):
            nc.vector.memset(negmax_parts[:, :], 0.0).then_inc(casts_ready, 1)
            for hf in range(2):
                for t in range(4 * hf, 4 * hf + 4):
                    if t % 2 == 0:
                        dve.wait_ge(x_in[t // 2], 16)
                    nc.vector.bn_stats(stats[:, t, :], resid[:, t, :]).then_inc(stats_ready, 1)
                for t in range(4 * hf, 4 * hf + 4):
                    dve.wait_ge(stats_ready, t + 1)
                    nc.vector.bn_aggr(mv[:, t, :], stats[:, t, :]).then_inc(mv_ready, 1)
                dve.wait_ge(mv_ready, 4 * hf + 4)
                nc.vector.tensor_scalar(veps[:, 4 * hf:4 * hf + 4], mv[:, 4 * hf:4 * hf + 4, 1], EPS, None,
                                        ALU.add).then_inc(veps_ready, 1)
            for hf in range(2):
                dve.wait_ge(rstd_ready, hf + 1)
                for t in range(4 * hf, 4 * hf + 4):
                    nc.vector.tensor_scalar(xn[:, t, :], resid[:, t, :], mv[:, t, 0:1], rstd[:, t:t + 1],
                                            ALU.subtract, ALU.mult).then_inc(xn_ready, 1)
            for hf in range(2):
                dve.wait_ge(xt_psum, 2 * hf + 2)
                nc.vector.tensor_copy(x_t[:, 1, hf * HALF:(hf + 1) * HALF], ps[:, 2 * hf + 1, :]).then_inc(xt_ready_v, 1)
            nc.vector.tensor_copy(ident_bf[:, :], ident).then_inc(casts_ready, 1)
            nc.vector.tensor_copy(before_bf[:, :], before).then_inc(casts_ready, 1)
            for n in range(5):
                if n < 4:
                    s, c = UP[n]
                    dve.wait_ge(high_ready, n + 1)
                    if n >= 2:
                        dve.wait_ge(mid_ready, n - 1)
                        dve.wait_ge(res2_ready, n - 1)
                    nc.vector.tensor_tensor(res1[n % 2], plain[:, s, c * HALF:(c + 1) * HALF],
                                            parts[:, s, 0, c * HALF:(c + 1) * HALF], ALU.subtract).then_inc(res1_ready, 1)
                if n >= 1:
                    s, c = UP[n - 1]
                    dve.wait_ge(mid_ready, n)
                    if n >= 3:
                        dve.wait_ge(low_ready, n - 2)
                    nc.vector.tensor_tensor(res2[(n - 1) % 2], res1[(n - 1) % 2],
                                            parts[:, s, 1, c * HALF:(c + 1) * HALF], ALU.subtract).then_inc(res2_ready, 1)
            dve.wait_ge(rope_in, 32)

            for n in range(4):
                s, c = UP[n]
                tt = slice(c * HALF, (c + 1) * HALF)
                dve.wait_ge(swap_psum, n + 1)
                nc.vector.scalar_tensor_tensor(rot_b[n], ps[:, 2 + n, :], up_bias[:, 2 * s + 1:2 * s + 2], sin_t[:, tt],
                                               ALU.add, ALU.mult).then_inc(swap_read, 1)
                nc.vector.tensor_tensor(plain[:, s, tt], plain[:, s, tt], cos_t[:, tt], ALU.mult).then_inc(rot_a_ready, 1)
            dve.wait_ge(vw_in, 48)
            dve.wait_ge(ones_ready, 2)
            for t in range(NT):
                dve.wait_ge(v_psum, 2 * (t // 2) + 2)
                for r in range(2):
                    groups = "p (g r j d) -> p g r j d"
                    nc.vector.tensor_tensor(v_ones[:, r::2, t, :, r * HD:(r + 1) * HD],
                                            ps[:, (6 + t // 2) % 8, (t % 2) * H:(t % 2) * H + H].rearrange(groups, r=2, j=GH, d=HD)[:, :, r],
                                            v_bias.rearrange(groups, r=2, j=GH, d=HD)[:, :, r], ALU.add).then_inc(v_ready, 1)

            steps = 0

            def route(ins):
                nonlocal steps
                steps += 1
                ins.then_inc(route_step, 1)
                dve.wait_ge(route_step, steps)

            dve.wait_ge(lg_psum, NT)
            route(nc.vector.tensor_copy(lg, ps[:, 4, 0:NT * E].rearrange("p (t e) -> p t e", t=NT)))
            nc.vector.tensor_reduce(top, lg, AX.X, ALU.max).then_inc(top_ready, 1)
            dve.wait_ge(top_ready, 1)
            route(nc.vector.tensor_tensor(pick, lg, top.unsqueeze(2).to_broadcast([P, NT, E]), ALU.is_equal))
            route(nc.vector.tensor_tensor(pick2, pick, weight_of, ALU.mult))
            route(nc.vector.tensor_reduce(pickmax, pick2, AX.X, ALU.max))
            route(nc.vector.tensor_tensor(onehot, pick2, pickmax.unsqueeze(2).to_broadcast([P, NT, E]), ALU.is_equal))
            nc.vector.tensor_copy(onehot_bf, onehot.rearrange("p t e -> p (t e)")).then_inc(onehot_ready, 1)
            dve.wait_ge(esc_ready, 1)
            route(nc.vector.tensor_scalar(esc1[:, :], esc[:, :], 1.0, None, ALU.add))
            nc.vector.reciprocal(score[:, :], esc1[:, :]).then_inc(score_ready, 1)
            dve.wait_ge(rank_psum, 1)
            nc.vector.tensor_copy(ranks.rearrange("p a t e -> p (a t e)"), ps[:, 5, 0:2 * NT * E]).then_inc(ranks_ready, 1)
            route(nc.vector.memset(passed[:, 0, :], 0.0))
            dve.wait_ge(ranks_ready, 1)
            for t in range(NT):
                route(nc.vector.tensor_tensor(passed[:, t + 1, :], passed[:, t, :], ranks[:, 1, t, :], ALU.add))
            route(nc.vector.tensor_tensor(cmp3, passed[:, NT, :].unsqueeze(2).to_broadcast([P, E, E]), steps_128, ALU.is_gt))
            route(nc.vector.tensor_reduce(tiles_of, cmp3, AX.X, ALU.add))
            route(nc.vector.tensor_tensor(cmp3, tiles_of.unsqueeze(1).to_broadcast([P, E, E]), earlier, ALU.mult))
            route(nc.vector.tensor_reduce(start_of, cmp3, AX.X, ALU.add))
            route(nc.vector.tensor_tensor(end_of, start_of, tiles_of, ALU.add))
            route(nc.vector.tensor_tensor(cmpj, end_of.unsqueeze(1).to_broadcast([P, TILES, E]), tile_no, ALU.is_le))
            route(nc.vector.tensor_reduce(tile_exp, cmpj, AX.X, ALU.add))
            route(nc.vector.tensor_scalar(tile_exp_i[:, :], tile_exp, float(E - 1), None, ALU.min))
            route(nc.vector.tensor_tensor(pick, passed[:, 0:NT, :], ranks[:, 0, :, :], ALU.add))
            route(nc.vector.scalar_tensor_tensor(pick2, start_of.unsqueeze(1).to_broadcast([P, NT, E]), float(P),
                                                 pick, ALU.mult, ALU.add))
            route(nc.vector.tensor_tensor(pick, pick2, onehot, ALU.mult))
            route(nc.vector.tensor_reduce(dest, pick, AX.X, ALU.add))
            nc.vector.tensor_copy(dest_i[:, :], dest).then_inc(dest_ready, 1)

            def row_max(n, c, i, b):
                dve.wait_ge(max_scores, n + 1)
                nc.vector.tensor_reduce(negmax[:, c, bass.ds(i, 1)], ps[:, 2 + 2 * b:4 + 2 * b, :], AX.XY,
                                        ALU.max, negate=True).then_inc(max_read, 1)

            def negmax_cut(m, c):
                src = negmax[:, c, :]
                dve.wait_ge(max_read, 16 * (m + 1))
                if not isinstance(m, int) or m > 0:
                    dve.wait_ge(negmax_turned, m)
                nc.vector.tensor_copy(negmax_parts[:, 0:16], src).then_inc(split_step, 1)
                dve.wait_ge(split_step, 4 * m + 1)
                nc.vector.tensor_tensor(split1[:, :], src, negmax_parts[:, 0:16], ALU.subtract).then_inc(split_step, 1)
                dve.wait_ge(split_step, 4 * m + 2)
                nc.vector.tensor_copy(negmax_parts[:, 16:32], split1[:, :]).then_inc(split_step, 1)
                dve.wait_ge(split_step, 4 * m + 3)
                nc.vector.tensor_tensor(split2[:, :], split1[:, :], negmax_parts[:, 16:32], ALU.subtract).then_inc(split_step, 1)
                dve.wait_ge(split_step, 4 * m + 4)
                nc.vector.tensor_copy(negmax_parts[:, 32:48], split2[:, :]).then_inc(negmax_split, 1)

            for n in range(AHEAD):
                row_max(n, n // 16, n % 16, n % 2)
                if n == 15:
                    negmax_cut(0, 0)

            def invert(n):
                nc.vector.reciprocal(den[:, bass.ds(n * P, P)], den[:, bass.ds(n * P, P)]).then_inc(inverted, 1)

            def to_numerators(k):
                dve.wait_ge(inverted, 4 * (k + 1))
                if k >= 1:
                    dve.wait_ge(attn_ready, 2 + k)
                nc.vector.memset(wait_slot[:, :], 0.0)
                nc.vector.stream_shuffle(rden[:, :], den[:, :], [(i + HD) % STRIP for i in range(STRIP)]).then_inc(rden_ready, 1)

            pairs_done = 0
            for m in range(2 * NG):
                c = m % 2
                if m + 1 < 2 * NG:
                    with dve.Fori(4, 8) as i:
                        row_max(16 * (m + 1) + 2 * i, 1 - c, 2 * i, 0)
                        row_max(16 * (m + 1) + 2 * i + 1, 1 - c, 2 * i + 1, 1)
                    negmax_cut(m + 1, 1 - c)
                inverts = m in (3, 4, 7)
                if inverts:
                    dve.wait_ge(den_ready, pairs_done + 1)
                if m + 2 < 2 * NG:
                    with dve.Fori(0, 4) as i:
                        row_max(16 * (m + 2) + 2 * i, c, 2 * i, 0)
                        row_max(16 * (m + 2) + 2 * i + 1, c, 2 * i + 1, 1)
                        if inverts:
                            invert(i)
                elif inverts:
                    for n in range(4):
                        invert(n)
                if inverts:
                    to_numerators(pairs_done)
                    pairs_done += 1
            def token_sum(t):
                dve.wait_ge(token_psum, t + 1)
                nc.vector.tensor_tensor(resid[:, t, :], ps[:, 6 + t % 2, 0:H], resid[:, t, :], ALU.add).then_inc(token_summed, 1)

            for t in range(EARLY):
                token_sum(t)

            def xt_copy(i):
                dve.wait_ge(tile_turned, i + 1)
                nc.vector.tensor_copy(tile_xt, ps[:, 2, 0:H].rearrange("p (k t) -> p k t", k=KH)).then_inc(tile_xt_ready, 1)

            def gate_up_product(i):
                dve.wait_ge(tile_gate_ready, i + 1)
                nc.vector.tensor_tensor(tile_h, ps[:, 1, :], tile_gate, ALU.mult).then_inc(tile_h_ready, 1)

            xt_copy(0)
            dve.wait_ge(den_ready, 4)
            for n in range(4):
                invert(n)
            to_numerators(3)
            with dve.Fori(0, TILES - 1) as i:
                dve.wait_ge(tile_gu_psum, i + 1)
                xt_copy(i + 1)
                gate_up_product(i)
            gate_up_product(TILES - 1)
            for t in range(NT):
                if t < NT - EARLY:
                    token_sum(EARLY + t)
                dve.wait_ge(gathered_in[t], 16)
                dve.wait_ge(token_summed, t + 1)
                nc.vector.tensor_tensor(resid[:, t, :], resid[:, t, :], gathered[:, t, :], ALU.add).then_inc(final_ready, 1)

        @block.gpsimd
        def _(pool):
            nc.gpsimd.memset(minus_half[:, :], -0.5).then_inc(half_set, 1)
            nc.gpsimd.memset(probs_w[:, 0:H], 0.0).then_inc(zero_set, 1)
            nc.gpsimd.memset(ones_bf[:, :], 1.0).then_inc(ones_ready, 1)
            pool.wait_ge(half_set, 1)
            for hf in range(2):
                pool.wait_ge(veps_ready, hf + 1)
                nc.gpsimd.tensor_tensor(rstd[:, 4 * hf:4 * hf + 4], veps[:, 4 * hf:4 * hf + 4],
                                        minus_half[:, 4 * hf:4 * hf + 4], ALU.pow).then_inc(rstd_ready, 1)
            nc.gpsimd.memset(v_ones[:, :, :, :, :], 1.0).then_inc(ones_ready, 1)
            pool.wait_ge(zero_set, 1)
            pool.dma_start(sorted_x.rearrange("(i p) d -> p i d", p=P),
                           probs_w[:, 0:H].unsqueeze(1).to_broadcast([P, TILES, H])).then_inc(zeros_in, 16)
            pool.wait_ge(vw_in, 48)
            for t in range(NT):
                pool.wait_ge(xn_ready, t + 1)
                nc.gpsimd.tensor_tensor(resid[:, t, :], resid[:, t, :], out_bias, ALU.add).then_inc(bias_added, 1)
            def shared_unit(u):
                fc, c = u % 4, u // 4
                pool.wait_ge(gu_read, 2 * u + 2)
                nc.gpsimd.tensor_tensor(hid[:, fc, c * HALF:(c + 1) * HALF], sh_gate[u % 2], sh_up[u % 2], ALU.mult)\
                    .then_inc(hid_ready, 1)

            for n in range(4):
                s, c = UP[n]
                tt = slice(c * HALF, (c + 1) * HALF)
                pool.wait_ge(rot_a_ready, n + 1)
                pool.wait_ge(swap_read, n + 1)
                nc.gpsimd.tensor_tensor(plain[:, s, tt], plain[:, s, tt], rot_b[n], ALU.add).then_inc(rot_ready, 1)
                shared_unit(2 * n)
                pool.wait_ge(high_ready, 5 + n)
                pool.wait_ge(mid_ready, 3 + n)
                pool.wait_ge(res2_ready, 3 + n)
                nc.gpsimd.tensor_tensor(res1[n % 2], plain[:, s, tt], parts[:, s, 0, tt], ALU.subtract).then_inc(res1_ready, 1)
                shared_unit(2 * n + 1)
                pool.wait_ge(mid_ready, 5 + n)
                pool.wait_ge(low_ready, 3 + n)
                nc.gpsimd.tensor_tensor(res2[n % 2], res1[n % 2], parts[:, s, 1, tt], ALU.subtract).then_inc(res2_ready, 1)
            pool.wait_ge(score_ready, 1)
            pool.wait_ge(xt_psum, 4)
            for t in range(NT):
                nc.gpsimd.tensor_scalar(xn[:, t, :], xn[:, t, :], score[:, t:t + 1], None, ALU.mult).then_inc(scaled_ready, 1)
            pool.wait_ge(zeros_in, 16)
            for i in range(2):
                nc.gpsimd.memset(token_pool[:, i:i + 1], 0.0).then_inc(attn_ready, 1)
            pool.wait_ge(dest_ready, 1)
            pool.wait_ge(scaled_ready, NT)
            for t in range(NT):
                pool.indirect_dma_start(out=sorted_x[:, :], out_offset=bass.IndirectOffsetOnAxis(ap=dest_i[:, t:t + 1], axis=0),
                                        in_=xn[:, t, :], in_offset=None).then_inc(scattered, 16)

            for k in range(4):
                r, c = k // 2, k % 2
                out_rows = attn[:, r, c * HALF:(c + 1) * HALF]
                pool.wait_ge(acc_read, 2 * (2 + 4 * r + 2 + c + 1))
                if k >= 1:
                    pool.wait_ge(rden_ready, k)
                nc.gpsimd.tensor_tensor(den[:, :], acc_sb[:, 0, c, 1, :], acc_sb[:, 1, c, 1, :], ALU.add).then_inc(den_ready, 1)
                nc.gpsimd.tensor_tensor(out_rows, acc_sb[:, 0, c, 0, :], acc_sb[:, 1, c, 0, :], ALU.add).then_inc(num_ready, 1)
                pool.wait_ge(num_ready, k + 1)
                pool.wait_ge(rden_ready, k + 1)
                nc.gpsimd.tensor_tensor(out_rows, out_rows, rden[:, :], ALU.mult).then_inc(attn_ready, 1)

            pool.wait_ge(tile_out, 16 * TILES)
            for t in range(NT):
                pool.indirect_dma_start(out=gathered[:, t, :], out_offset=None, in_=sorted_y[:, :],
                                        in_offset=bass.IndirectOffsetOnAxis(ap=dest_i[:, t:t + 1], axis=0)).then_inc(gathered_in[t], 16)

        @block.tensor
        def _(pe):
            pe.wait_ge(consts_in, 16)
            for hf in range(2):
                pe.wait_ge(xn_ready, 4 * hf + 4)
                for k in range(KH):
                    for t in range(4):
                        last = pe.transpose(ps[:, 2 * hf + k, t * P:(t + 1) * P], xn[:, 4 * hf + t, k::KH], ident)
                    last.then_inc(xt_psum, 1)
            pe.wait_ge(latw_in, 32)
            for c in range(2):
                pe.wait_ge(xt_ready_a, c + 1)
                pe.wait_ge(xt_ready_v, c + 1)
                for k in range(KH):
                    last = pe.matmul(ps[:, 4 + c, :], lat_wt[:, k, :], x_t[:, k, c * HALF:(c + 1) * HALF],
                                     start=(k == 0), stop=(k == KH - 1))
                last.then_inc(lat_psum, 1)
            pe.wait_ge(upw_in, 48)
            for w in range(2):
                for n in range(4):
                    s, c = UP[n]
                    pe.wait_ge(lat_ready, c + 1)
                    bank = 2 + n if w else (6 + n) % 8
                    pe.matmul(ps[:, bank, :], up_wt[:, (2 * s + w) * P:(2 * s + w + 1) * P], lat[:, c * HALF:(c + 1) * HALF],
                              start=True, stop=True).then_inc(swap_psum if w else up_psum, 1)
            pe.wait_ge(vw_in, 48)
            pe.wait_ge(plain_ready, 4)
            for t in range(NT):
                pe.matmul(ps[:, (6 + t // 2) % 8, (t % 2) * H:(t % 2) * H + H], lat[:, t * P:(t + 1) * P], v_wt,
                          start=True, stop=True).then_inc(v_psum, 1)
            pe.wait_ge(router_in, 16)
            pe.wait_ge(swap_read, 4)
            for c in range(2):
                for k in range(KH):
                    last = pe.matmul(ps[0:E, 2 + c, :], router_t[:, k, :], x_t[:, k, c * HALF:(c + 1) * HALF],
                                     start=(k == 0), stop=(k == KH - 1))
                last.then_inc(lgt_psum, 1)
            pe.wait_ge(lgt_ready, 2)
            for t in range(NT):
                pe.transpose(ps[:, 4, t * E:(t + 1) * E], logit_t[0:E, t * P:(t + 1) * P], ident[0:E, 0:E]).then_inc(lg_psum, 1)
            pe.wait_ge(onehot_ready, 1)
            pe.wait_ge(casts_ready, 3)
            pe.wait_ge(ones_ready, 2)
            pe.matmul(ps[:, 5, 0:NT * E], before_bf[:, :], onehot_bf, start=True, stop=True)
            pe.matmul(ps[:, 5, NT * E:2 * NT * E], ones_bf[:, :], onehot_bf, start=True, stop=True).then_inc(rank_psum, 1)

            def max_tile(n):
                c, g, j, qt = n // 16 % 2, n // 32, n % 16 // 4, n % 4
                if n % 32 == 0 and g > 0:
                    pe.wait_ge(stacks_in[g], 16 * STACK_LOADS)
                if n >= 2:
                    pe.wait_ge(max_read, n - 1)
                for kh in range(2):
                    last = pe.matmul(ps[:, 2 + 2 * (n % 2) + kh, :],
                                     q_stack[0:KROWS, g, c, j, qt * P:(qt + 1) * P],
                                     k_stack[0:KROWS, g, j, kh * HALF:(kh + 1) * HALF], start=True, stop=True)
                last.then_inc(max_scores, 1)

            def negmax_turn(m, c):
                pe.wait_ge(negmax_split, m + 1)
                pe.transpose(ps[:, 6 + c, 0:64].bitcast(BF16), negmax_parts[:, :], ident_bf[:, :]).then_inc(negmax_turned, 1)

            fc_units = [(u % 4, u // 4) for u in range(8)]
            maxima = iter(range(AHEAD))
            pe.wait_ge(v_ready, 2 * NT)
            pe.wait_ge(sgu_in, 16)
            for u, (fc, c) in enumerate(fc_units):
                b = 0 if u % 2 == 0 else 6
                if u == 2:
                    pe.wait_ge(ranks_ready, 1)
                    pe.wait_ge(stacks_in[0], 16 * STACK_LOADS)
                if u >= 2:
                    pe.wait_ge(gu_read, 2 * (u - 1))
                if u == 7:
                    pe.wait_ge(negmax_copied, 1)
                for w in range(2):
                    for k in range(KH):
                        if (u, w, k) == (6, 1, 1):
                            pe.wait_ge(gu_read, 12)
                            negmax_turn(0, 0)
                        last = pe.matmul(ps[:, b + w, :], sgu[:, k, w * F + fc:(w + 1) * F:KF],
                                         x_t[:, k, c * HALF:(c + 1) * HALF], start=(k == 0), stop=(k == KH - 1))
                        if u == 7 and k == 0:
                            last.then_inc(probs_used, 1)
                        if k == KH - 1 and w == 1:
                            last.then_inc(gu_psum, 1)
                        if u >= 2:
                            max_tile(next(maxima))
            assert next(maxima, None) is None
            pe.wait_ge(gu_read, 16)

            def score_tile(g, c, kt, j):
                n = GH * (NT * (2 * g + c) + kt) + j
                pe.wait_ge(probs_ready, n + 1)
                pe.matmul(ps[:, j % 2, :], k_stack[0:ROWS, g, j, kt * P:(kt + 1) * P], q_stack[0:ROWS, g, c, j, :],
                          start=True, stop=True).then_inc(scores_psum, 1)

            def weigh(g, c, kt):
                step = NT * (2 * g + c) + kt
                pe.wait_ge(probs_ready, GH * step + GH + 2)
                for j in range(GH):
                    last = pe.matmul(ps[STRIP * j:STRIP * j + STRIP, 6 + c, :], v_ones[:, g, kt, j, :], probs[:, kt % 2, j, :],
                                     start=(kt == 0), stop=(kt == NT - 1))
                last.then_inc(probs_used, 1)

            maxima = iter(range(AHEAD, 2 * NG * 16))
            for m in range(2 * NG):
                g, c = m // 2, m % 2
                pe.wait_ge(negmax_in, 48 * (m + 1))
                for kt in range(NT):
                    score_tile(g, c, kt, 0)
                    score_tile(g, c, kt, 1)
                    if kt == 1:
                        pe.wait_ge(acc_read, 2 * (m + 1))
                        pe.wait_ge(negmax_copied, m + 1)
                    if kt >= 1:
                        weigh(g, c, kt - 1)
                    elif m >= 1:
                        weigh((m - 1) // 2, 1 - c, NT - 1)
                    score_tile(g, c, kt, 2)
                    score_tile(g, c, kt, 3)
                    if kt == 5 and m + 1 < 2 * NG:
                        pe.wait_ge(acc_read, 2 * (m + 2))
                        negmax_turn(m + 1, 1 - c)
                    for n in (next(maxima, None), next(maxima, None)):
                        if n is not None:
                            max_tile(n)
            weigh(NG - 1, 1, NT - 1)

            pe.wait_ge(tail_in, 32)
            pe.wait_ge(hid_ready, 8)
            pe.wait_ge(attn_ready, 2 + 3)
            pe.wait_ge(acc_read, 2 * (2 + 2 * NG))

            def token_tile(t):
                if t >= 2:
                    pe.wait_ge(token_summed, t - 1)
                tt = slice(t * P, (t + 1) * P)
                for k in range(KF):
                    pe.matmul(ps[:, 6 + t % 2, 0:H], hid[:, k, tt], sdn[:, k, :], start=(k == 0), stop=False)
                for r in range(2):
                    last = pe.matmul(ps[:, 6 + t % 2, 0:H], attn[:, r, tt], wout[:, r, :], start=False, stop=(r == 1))
                last.then_inc(token_psum, 1)

            for t in range(EARLY):
                token_tile(t)

            def turn_tile(i):
                pe.wait_ge(tile_in, 16 * (i + 1))
                for k in range(KH):
                    last = pe.transpose(ps[:, 2, k * P:(k + 1) * P], tile_x[:, k::KH], ident)
                last.then_inc(tile_turned, 1)

            def expert_of(i):
                return pe.value_load(tile_exp_i[0:1, bass.ds(i, 1)], min_val=0, max_val=E - 1)

            def weights(e, at_, n):
                return exp_w[:, bass.ds(e, 1), at_:at_ + n].rearrange("p o n -> p (o n)")

            def gate_up_tile(i, e):
                pe.wait_ge(tile_xt_ready, i + 1)
                for w in range(2):
                    for k in range(KH):
                        last = pe.matmul(ps[:, w, :], tile_xt[:, k, :], weights(e, k * GU + w * F, F),
                                         start=(k == 0), stop=(k == KH - 1))
                last.then_inc(tile_gu_psum, 1)

            def turn_h(i):
                pe.wait_ge(tile_h_ready, i + 1)
                for k in range(KF):
                    last = pe.transpose(ps[:, 3, k * P:(k + 1) * P], tile_h[:, k::KF], ident)
                last.then_inc(tile_ht_psum, 1)

            def down_tile(i, e):
                pe.wait_ge(tile_ht_ready, i + 1)
                for k in range(KF):
                    last = pe.matmul(ps[:, 5, 0:H], tile_ht[:, k, :], weights(e, KH * GU + k * H, H),
                                     start=(k == 0), stop=(k == KF - 1))
                last.then_inc(tile_y_psum, 1)

            pe.wait_ge(exp_low_in, 16 * E)
            pe.wait_ge(exp_high_in, 16 * E)
            turn_tile(0)
            gate_up_tile(0, expert_of(0))
            turn_tile(1)
            e_next = expert_of(1)
            turn_h(0)
            gate_up_tile(1, e_next)
            with pe.Fori(1, TILES - 1) as i:
                turn_tile(i + 1)
                down_tile(i - 1, expert_of(i - 1))
                e_next = expert_of(i + 1)
                turn_h(i)
                gate_up_tile(i + 1, e_next)
            pe.wait_ge(tile_y_ready, TILES - 2)
            down_tile(TILES - 2, expert_of(TILES - 2))
            turn_h(TILES - 1)
            pe.wait_ge(tile_y_ready, TILES - 1)
            down_tile(TILES - 1, expert_of(TILES - 1))
            pe.wait_ge(attn_ready, 2 + 4)
            for t in range(EARLY, NT):
                token_tile(t)


def _constants():
    ident = np.eye(P, dtype=np.float32)
    before = np.triu(np.ones((P, P), np.float32), 1)
    weight_of = np.tile(np.arange(E, 0, -1, dtype=np.float32), NT)
    steps_128 = np.tile(P * np.arange(E, dtype=np.float32), E)
    earlier = np.tril(np.ones((E, E), np.float32), -1).reshape(-1)
    tile_no = np.repeat(np.arange(TILES, dtype=np.float32), E)
    row = np.concatenate([weight_of, steps_128, earlier, tile_no])
    first = (np.arange(P) % STRIP < HD).astype(np.float32)[:, None]
    return np.concatenate([ident, before, np.tile(row, (P, 1)), first, 1 - first, first], 1)


def _rope():
    dim = H // 4
    inv = (np.float32(1) / np.float32(10000.0) ** (np.arange(0, dim, 2, dtype=np.float32) / np.float32(dim))).astype(np.float32)
    freq = np.outer(np.arange(T, dtype=np.float32), inv).astype(np.float32).T
    cos, sin = np.cos(freq).astype(np.float32), np.sin(freq).astype(np.float32)
    return np.concatenate([cos] * 4), np.concatenate([-sin, -sin, sin, sin])


def kernel(**inputs):
    import concourse.bacc as bacc
    from concourse.bass_utils import run_bass_kernel_spmd

    a = {k.split("_", 1)[1]: np.asarray(v) for k, v in inputs.items()}
    swap = np.r_[64:128, 0:64]
    wq, wk = a["attn_Wq_up"].T, a["attn_Wk_up"].T
    bq, bk = a["attn_bq_up"], a["attn_bk_up"]
    wo = a["attn_Wo"].T.reshape(2, 2, GH, HD, H).transpose(2, 1, 3, 0, 4)
    v_w = np.zeros((P, H), np.float32)
    v_w[64:] = a["attn_Wv_up"].T
    zero = np.zeros((LAT, P), np.float32)
    cos, sin = _rope()
    arrays = {
        "x": a["attn_hidden_states"].reshape(T, H),
        "lat_w": np.concatenate([a["attn_Wq_down"].T, a["attn_Wkv_down"].T], 1),
        "lat_b": np.concatenate([a["attn_bq_down"], a["attn_bkv_down"]])[:, None],
        "up_w": np.concatenate([np.concatenate([wq, wq[:, swap], zero, zero], 1), np.concatenate([zero, zero, wk, wk[:, swap]], 1)], 0),
        "up_b": np.stack([bq, bq[swap], bk, bk[swap]], 1),
        "v_w": v_w,
        "v_b": a["attn_bv_up"],
        "rope_c": cos,
        "rope_s": sin,
        "router_w": a["ffn_router_w"].T,
        "sgu_w": np.concatenate([a["ffn_shared_gate_w"], a["ffn_shared_up_w"]], 1),
        "sdn_w": a["ffn_shared_down_w"],
        "out_w": wo.reshape(P, 2, H),
        "out_b": a["attn_bo"],
        "gate_up": a["ffn_gate_up_proj"],
        "down": a["ffn_down_proj"],
        "consts": _constants(),
        "one_rows": np.ones((ROWS - KROWS, NH, T), mybir.dt.np(BF16)),
    }
    nc = bacc.Bacc("TRN2", target_bir_lowering=False, num_devices=1)
    args = []
    for name, value in arrays.items():
        arrays[name] = np.ascontiguousarray(value)
        args.append(nc.dram_tensor(name, arrays[name].shape, mybir.dt.from_np(arrays[name].dtype), kind="ExternalInput").ap())
    out = nc.dram_tensor("out", [T, H], F32, kind="ExternalOutput").ap()
    build_kernel(nc, *args, out)
    result = run_bass_kernel_spmd(nc, [arrays], core_ids=[0])
    return result.results[0]["out"].reshape(1, T, H)
```

```python
from contextlib import ExitStack

import numpy as np

import concourse.bass as bass
from concourse import mybir

F32 = mybir.dt.float32
BF16 = mybir.dt.bfloat16
I32 = mybir.dt.int32
ALU = mybir.AluOpType
ACT = mybir.ActivationFunctionType
AX = mybir.AxisListType

P = 128
T, H = 1024, 256
NH, HD, LAT = 16, 16, 64
E, F = 8, 512
EPS = 1e-5
NT = T // P
KH, KF = H // P, F // P
GH = 4
NG = NH // GH
HALF = T // 2
STRIP = P // GH
PARTS_Q = (0, 0, 0, 1, 1, 2)
PARTS_K = (0, 1, 2, 0, 1, 0)
KROWS = len(PARTS_Q) * HD
ROWS = KROWS + 3
TILES = T // P + E - 1
EARLY = 2
GU = 2 * F
WEXP = KH * GU + KF * H

STACK = GH * T
STACKS_AT = (E // 2) * WEXP
ARENA = STACKS_AT + NG * STACK
STACK_LOADS = (12, 6)
V_BANKS = (4, 5, 2, 3)
WARM_UP = 16
MAXIMA_AFTER = ((0, 0, 0, 0),) * 4 + ((1, 2, 1, 2),) * 3 + ((1, 1, 1, 0),)
LEAD = 3
WIDE = 2 * NG * NT - 12
AHEAD = 24
UP = ((1, 0), (0, 0), (1, 1), (0, 1))


def build_kernel(nc, x, lat_w, lat_b, up_w, up_b, v_w, v_b, rope_c, rope_s, router_w, sgu_w, sdn_w,
                 out_w, out_b, gate_up, down, consts, one_rows, out):
    nc.disable_value_cache = True
    ctx = ExitStack()
    with ctx:
        def sb(name, shape, dt=F32):
            return ctx.enter_context(nc.sbuf_tensor(name, shape, dt))

        def sem(name):
            return ctx.enter_context(nc.semaphore(name))

        ps = ctx.enter_context(nc.psum_tensor("ps", [P, 8, 512], F32))

        part_dram = [nc.dram_tensor(f"parts_{s}", [3, 2, P, T], BF16, kind="Internal").ap() for s in "qk"]
        sorted_x = nc.dram_tensor("sorted_x", [TILES * P, H], F32, kind="Internal").ap()
        sorted_y = nc.dram_tensor("sorted_y", [TILES * P, H], F32, kind="Internal").ap()

        arena = sb("arena", [P, ARENA])
        resid = sb("resid", [P, NT, H])
        v_ones = sb("v_ones", [P, NG, NT, GH, STRIP])
        probs = sb("probs", [P, 2, GH, HALF])
        work = sb("work", [P, 6 * T])
        hid = sb("hid", [P, KF, T])
        den = sb("den", [P, 4, HALF])
        rden = sb("rden", [P, HALF])
        cst = sb("cst", [P, 2 * P + 3 * 64 + TILES * E + 3])
        ident_bf = sb("ident_bf", [P, P], BF16)
        before_bf = sb("before_bf", [P, P], BF16)
        ones_bf = sb("ones_bf", [P, P], BF16)
        lat_bias = sb("lat_bias", [P, 1])
        up_bias = sb("up_bias", [P, 2])
        stats = sb("stats", [P, NT, 6])
        mv = sb("mv", [P, NT, 2])
        veps = sb("veps", [P, NT])
        minus_half = sb("minus_half", [P, NT])
        rstd = sb("rstd", [P, NT])
        token_pool = sb("token_pool", [P, 2])
        tile_x = sb("tile_x", [P, H])
        wait_slot = sb("wait_slot", [P, 1])
        token_act = sb("token_act", [P, 4])
        negmax = sb("negmax", [P, 2, GH * 4])
        split1 = sb("split1", [P, GH * 4])
        split2 = sb("split2", [P, GH * 4])
        negmax_parts = sb("negmax_parts", [P, P], BF16)
        negmax_rows = sb("negmax_rows", [3 * GH * 4, P], BF16)
        tile_exp_i = sb("tile_exp_i", [P, TILES], I32)
        dest_i = sb("dest_i", [P, NT], I32)
        esc = sb("esc", [P, NT])
        esc1 = sb("esc1", [P, NT])
        score = sb("score", [P, NT])

        def words(at, n):
            return arena[:, at:at + n]

        stacks = words(STACKS_AT, NG * STACK).bitcast(BF16).rearrange("p (g n) -> p g n", g=NG)
        q_stack = stacks[:, :, 0:STACK].rearrange("p g (c h t) -> p g c h t", c=2, h=GH)
        k_stack = stacks[:, :, STACK:2 * STACK].rearrange("p g (h t) -> p g h t", h=GH)
        exp_w = words(0, E * WEXP).rearrange("p (e n) -> p e n", e=E)
        at = 0

        def temp(n):
            nonlocal at
            at += n
            return words(at - n, n)

        cos_t, sin_t = temp(T), temp(T)
        plain = temp(2 * T).rearrange("p (s t) -> p s t", s=2)
        parts = temp(2 * 3 * T // 2).bitcast(BF16).rearrange("p (s a t) -> p s a t", s=2, a=3)
        lat = temp(T)
        logit_t = temp(T)
        lat_wt = temp(KH * P).rearrange("p (k n) -> p k n", k=KH)
        up_wt = temp(2 * P)
        v_wt = temp(H)
        v_bias = temp(H)
        out_bias = temp(H)
        router_t = temp(KH * E).rearrange("p (k e) -> p k e", k=KH)
        te = "p (t e) -> p t e"
        lg, pick, pick2, onehot = [temp(NT * E).rearrange(te, t=NT) for _ in range(4)]
        top, pickmax, dest = temp(NT), temp(NT), temp(NT)
        onehot_bf = temp(NT * E // 2).bitcast(BF16)
        ranks = temp(2 * NT * E).rearrange("p (a t e) -> p a t e", a=2, t=NT)
        passed = temp((NT + 1) * E).rearrange(te, e=E)
        cmp3 = temp(E * E).rearrange("p (e m) -> p e m", e=E)
        tiles_of, start_of, end_of = temp(E), temp(E), temp(E)
        cmpj = temp(TILES * E).rearrange(te, e=E)
        tile_exp = temp(TILES)
        assert at <= STACKS_AT, at

        v_words = v_ones[:, 0:2, :, :, :].rearrange("p g t j d -> p (g t j d)")
        sdn = v_words[:, 0:KF * H].rearrange("p (k n) -> p k n", k=KF)
        wout = v_words[:, KF * H:KF * H + 2 * H].rearrange("p (g n) -> p g n", g=2)
        tile_xt = v_words[:, KF * H + 2 * H:][:, 0:H].rearrange("p (k t) -> p k t", k=KH)

        attn = work[:, 4 * T:6 * T].rearrange("p (r t) -> p r t", r=2)
        x_t = work[:, 4 * T:6 * T].rearrange("p (k t) -> p k t", k=KH)
        sgu = work[:, 2 * T:4 * T].rearrange("p (k n) -> p k n", k=KH)
        xn = work[:, 0:2 * T].rearrange("p (t d) -> p t d", t=NT)
        acc_sb = work[:, 0:4 * T].rearrange("p (r c w n) -> p r c w n", r=2, c=2, w=2)
        gathered = xn
        probs_w = probs[:, :, :, :].rearrange("p a j t -> p (a j t)")
        sh_gate = [probs_w[:, 1024 * u:1024 * u + 512] for u in range(2)]
        sh_up = [probs_w[:, 1024 * u + 512:1024 * u + 1024] for u in range(2)]
        rot_b = [probs_w[:, 2048 + 512 * n:2560 + 512 * n] for n in range(4)]
        res = words(STACKS_AT + (NG - 1) * STACK, 4 * HALF).rearrange("p (u n) -> p u n", u=4)
        res1 = [res[:, u, :] for u in range(2)]
        res2 = [res[:, 2 + u, :] for u in range(2)]
        tile_gate = probs_w[:, 512:1024]
        tile_h = probs_w[:, 1024:1536]
        tile_ht = probs_w[:, 1536:2048].rearrange("p (k t) -> p k t", k=KF)
        tile_y = probs_w[:, 2048:2304]

        ident = cst[:, 0:P]
        before = cst[:, P:2 * P]
        c0 = 2 * P
        weight_of = cst[:, c0:c0 + 64].rearrange("p (t e) -> p t e", t=NT)
        steps_128 = cst[:, c0 + 64:c0 + 128].rearrange("p (e m) -> p e m", e=E)
        earlier = cst[:, c0 + 128:c0 + 192].rearrange("p (e m) -> p e m", e=E)
        tile_no = cst[:, c0 + 192:c0 + 192 + TILES * E].rearrange("p (j e) -> p j e", j=TILES)
        rows_of = cst[:, c0 + 192 + TILES * E:]

        x_in = [sem(f"x_in{i}") for i in range(4)]
        consts_in, latw_in, upw_in, rope_in = sem("consts_in"), sem("latw_in"), sem("upw_in"), sem("rope_in")
        vw_in, router_in, sgu_in, tail_in = sem("vw_in"), sem("router_in"), sem("sgu_in"), sem("tail_in")
        stats_ready, mv_ready, veps_ready = sem("stats_ready"), sem("mv_ready"), sem("veps_ready")
        rstd_ready, half_set = sem("rstd_ready"), sem("half_set")
        xn_ready, xt_psum, xt_ready_a, xt_ready_v = sem("xn_ready"), sem("xt_psum"), sem("xt_ready_a"), sem("xt_ready_v")
        casts_ready, ones_ready = sem("casts_ready"), sem("ones_ready")
        lat_psum, lat_ready = sem("lat_psum"), sem("lat_ready")
        up_psum, plain_ready, swapped = sem("up_psum"), sem("plain_ready"), sem("swapped")
        rot_a_ready, rot_ready = sem("rot_a_ready"), sem("rot_ready")
        high_ready, res1_ready, mid_ready = sem("high_ready"), sem("res1_ready"), sem("mid_ready")
        res2_ready, low_ready = sem("res2_ready"), sem("low_ready")
        parts_stored = [sem(f"parts_stored_{i}") for i in range(8)]
        stacks_in = [[sem(f"stacks_in{g}_{c}") for c in range(2)] for g in range(NG)]
        v_psum, v_ready = sem("v_psum"), sem("v_ready")
        lgt_psum, lgt_ready, lg_psum, lg_ready = sem("lgt_psum"), sem("lgt_ready"), sem("lg_psum"), sem("lg_ready")
        route_step, onehot_ready, rank_psum, ranks_ready = sem("route_step"), sem("onehot_ready"), sem("rank_psum"), sem("ranks_ready")
        top_ready, esc_ready, score_ready, dest_ready = sem("top_ready"), sem("esc_ready"), sem("score_ready"), sem("dest_ready")
        scaled_ready, zero_set, zeros_in, scattered = sem("scaled_ready"), sem("zero_set"), sem("zeros_in"), sem("scattered")
        bias_added = sem("bias_added")
        gu_psum, gu_read, hid_ready = sem("gu_psum"), sem("gu_read"), sem("hid_ready")
        max_scores, max_read = sem("max_scores"), sem("max_read")
        split_step, negmax_split, negmax_turned = sem("split_step"), sem("negmax_split"), sem("negmax_turned")
        negmax_copied, negmax_in = sem("negmax_copied"), sem("negmax_in")
        scores_psum, probs_ready, probs_used = sem("scores_psum"), sem("probs_ready"), sem("probs_used")
        acc_read, den_ready, rden_ready, attn_ready = sem("acc_read"), sem("den_ready"), sem("rden_ready"), sem("attn_ready")
        num_ready, inverted = sem("num_ready"), sem("inverted")
        exp_low_in, exp_high_in = sem("exp_low_in"), sem("exp_high_in")
        token_psum, token_summed = sem("token_psum"), sem("token_summed")
        tile_in, tile_turned, tile_xt_ready = sem("tile_in"), sem("tile_turned"), sem("tile_xt_ready")
        tile_gu_psum, tile_gate_ready, tile_h_ready = sem("tile_gu_psum"), sem("tile_gate_ready"), sem("tile_h_ready")
        tile_ht_psum, tile_ht_ready, tile_y_psum = sem("tile_ht_psum"), sem("tile_ht_ready"), sem("tile_y_psum")
        tile_y_ready, tile_out = sem("tile_y_ready"), sem("tile_out")
        gathered_in = [sem(f"gathered_in{t}") for t in range(NT)]
        routed_added = sem("routed_added")
        final_ready, stored = sem("final_ready"), sem("stored")

        x_dram = x.rearrange("(t p) d -> p t d", p=P)
        out_dram = out.rearrange("(t p) d -> p t d", p=P)

        def part_rows(s, a, b, g, c0, c1):
            rows = slice((g % 2) * GH * HD, (g % 2 + 1) * GH * HD)
            return part_dram[s][a:b, g // 2, rows, c0:c1].rearrange("a (h d) t -> a d h t", d=HD)

        def turn_bank(i):
            return 5 if isinstance(i, int) and i == 0 else 2

        block = ctx.enter_context(nc.Block())

        @block.sync
        def _(sp):
            sp.dma_start(resid[:, 0:2, :], x_dram[:, 0:2, :]).then_inc(x_in[0], 16)
            sp.dma_start(resid[:, 4:6, :], x_dram[:, 4:6, :]).then_inc(x_in[2], 16)
            sp.dma_start(cst[:, :], consts).then_inc(consts_in, 16)
            sp.dma_start(lat_wt, lat_w.rearrange("(p k) n -> p k n", k=KH)).then_inc(latw_in, 16)
            sp.dma_start(lat_bias[:, :], lat_b).then_inc(latw_in, 16)
            sp.dma_start(up_wt, up_w).then_inc(upw_in, 16)
            sp.dma_start(up_bias[:, :], up_b).then_inc(upw_in, 16)
            sp.dma_start(sgu, sgu_w.rearrange("(p k) n -> p k n", k=KH)).then_inc(sgu_in, 16)
            sp.dma_start(k_stack[KROWS:ROWS], one_rows.rearrange("r (g h) t -> r g h t", g=NG)).then_inc(upw_in, 16)
            sp.dma_start(router_t, router_w.rearrange("(p k) e -> p k e", k=KH)).then_inc(router_in, 16)

            def store_parts(n, octet):
                s, c = UP[n % 4]
                sp.wait_ge(low_ready, n + 1)
                sp.dma_start(part_dram[s][:, octet, :, c * HALF:(c + 1) * HALF].rearrange("a p t -> p a t"),
                             parts[:, s, :, c * HALF:(c + 1) * HALF]).then_inc(parts_stored[n], 16)

            def load_stacks(g):
                for row, n_parts in ((0, 3), (3, 2), (5, 1)):
                    for a in range(n_parts):
                        sp.dma_start(k_stack[HD * (row + a):HD * (row + a + 1), g, :, :],
                                     part_rows(1, a, a + 1, g, 0, T).rearrange("a d h t -> (a d) h t")).then_inc(stacks_in[g][0], 16)
                load_q(g, 0)

            def load_q(g, c):
                for row, a in enumerate(PARTS_Q):
                    sp.dma_start(q_stack[HD * row:HD * row + HD, g, c, :, :],
                                 part_rows(0, a, a + 1, g, c * HALF, (c + 1) * HALF).rearrange("a d h t -> (a d) h t"))\
                        .then_inc(stacks_in[g][c], 16)

            def negmax_load(m, g, c):
                sp.wait_ge(negmax_copied, m + 1)
                for a in range(3):
                    sp.dma_start(q_stack[KROWS + a:KROWS + a + 1, g, c, :, :].rearrange("p h t -> p (h t)"),
                                 negmax_rows[16 * a:16 * a + 16, :]).then_inc(negmax_in, 16)

            def load_expert(e, loaded):
                sp.dma_start(exp_w[:, e, 0:KH * GU], gate_up[e].rearrange("(p k) n -> p (k n)", k=KH)).then_inc(loaded, 16)
                sp.dma_start(exp_w[:, e, KH * GU:], down[e].rearrange("(p k) n -> p (k n)", k=KF)).then_inc(loaded, 16)

            for n in range(4):
                store_parts(n, 0)
            for n in range(3):
                sp.wait_ge(parts_stored[n], 16)
            load_stacks(0)
            sp.wait_ge(parts_stored[3], 16)
            load_q(0, 1)
            load_stacks(1)
            load_q(1, 1)
            for n in range(4, 8):
                if n == 7:
                    negmax_load(0, 0, 0)
                store_parts(n, 1)
            for n in range(4, 8):
                sp.wait_ge(parts_stored[n], 16)
            load_stacks(2)
            load_q(2, 1)
            negmax_load(1, 0, 1)
            load_stacks(3)
            load_q(3, 1)
            for g in range(1, NG):
                negmax_load(2 * g, g, 0)
                if g == 1:
                    sp.wait_ge(v_ready, 2 * NT)
                    sp.wait_ge(lg_psum, NT)
                    sp.wait_ge(bias_added, NT)
                    sp.wait_ge(dest_ready, 1)
                    sp.wait_ge(esc_ready, 1)
                    sp.wait_ge(rot_ready, 4)
                    for e in range(E // 2):
                        load_expert(e, exp_low_in)
                negmax_load(2 * g + 1, g, 1)
                sp.wait_ge(max_scores, 32 * g)
                sp.wait_ge(scores_psum, 2 * GH * NT * g)
                load_expert(E // 2 + g - 1, exp_high_in)
            load_expert(E - 1, exp_high_in)
            sp.wait_ge(probs_used, 2 + 4 * NT)
            sp.dma_start(sdn, sdn_w.rearrange("(p k) n -> p k n", k=KF)).then_inc(tail_in, 16)
            sp.dma_start(wout, out_w).then_inc(tail_in, 16)

            sp.wait_ge(scattered, 16 * NT)
            sp.dma_start(tile_x[:, :], sorted_x[0:P, :]).then_inc(tile_in, 16)
            with sp.Fori(1, TILES) as i:
                sp.wait_ge(tile_turned, i)
                sp.dma_start(tile_x[:, :], sorted_x[bass.ds(i * P, P), :]).then_inc(tile_in, 16)

            for t in range(NT):
                sp.wait_ge(final_ready, t + 1)
                sp.dma_start(out_dram[:, t, :], resid[:, t, :]).then_inc(stored, 16)
            sp.wait_ge(stored, 16 * NT)

        @block.scalar
        def _(act):
            act.dma_start(resid[:, 2:4, :], x_dram[:, 2:4, :]).then_inc(x_in[1], 16)
            act.dma_start(resid[:, 6:8, :], x_dram[:, 6:8, :]).then_inc(x_in[3], 16)
            act.dma_start(cos_t, rope_c).then_inc(rope_in, 16)
            act.dma_start(sin_t, rope_s).then_inc(rope_in, 16)
            act.dma_start(v_wt, v_w).then_inc(vw_in, 16)
            act.dma_start(v_bias, v_b.partition_broadcast(P)).then_inc(vw_in, 16)
            act.dma_start(out_bias, out_b.partition_broadcast(P)).then_inc(vw_in, 16)

            for hf in range(2):
                act.wait_ge(xt_psum, 2 * hf + 1)
                nc.scalar.copy(x_t[:, 0, hf * HALF:(hf + 1) * HALF], ps[:, 2 * hf, :]).then_inc(xt_ready_a, 1)
            act.wait_ge(latw_in, 32)
            for c in range(2):
                act.wait_ge(lat_psum, c + 1)
                nc.scalar.activation(lat[:, c * HALF:(c + 1) * HALF], ps[:, 4 + c, :], ACT.Identity,
                                     bias=lat_bias[:, 0:1]).then_inc(lat_ready, 1)
            act.wait_ge(upw_in, 48)

            def piece(n, a, src):
                s, c = UP[n % 4]
                return nc.scalar.copy(parts[:, s, a, c * HALF:(c + 1) * HALF], src)

            def middle(n):
                act.wait_ge(res1_ready, n + 1)
                piece(n, 1, res1[n % 2]).then_inc(mid_ready, 1)

            def low(n):
                act.wait_ge(res2_ready, n + 1)
                act.wait_ge(mid_ready, n + 1)
                act.wait_ge(high_ready, n + 1)
                piece(n, 2, res2[n % 2]).then_inc(low_ready, 1)

            for n in range(6):
                if n < 4:
                    s, c = UP[n]
                    act.wait_ge(up_psum, n + 1)
                    nc.scalar.activation(plain[:, s, c * HALF:(c + 1) * HALF], ps[:, (6 + n) % 8, :], ACT.Identity,
                                         bias=up_bias[:, s:s + 1]).then_inc(plain_ready, 1)
                    act.wait_ge(plain_ready, n + 1)
                    piece(n, 0, plain[:, s, c * HALF:(c + 1) * HALF]).then_inc(high_ready, 1)
                if 1 <= n < 5:
                    middle(n - 1)
                if n >= 2:
                    low(n - 2)

            def shared_unit(u):
                b = 0 if u % 2 == 0 else 6
                act.wait_ge(gu_psum, u + 1)
                if u >= 2:
                    act.wait_ge(hid_ready, u - 1)
                nc.scalar.activation(sh_gate[u % 2], ps[:, b, :], ACT.Silu).then_inc(gu_read, 1)
                nc.scalar.copy(sh_up[u % 2], ps[:, b + 1, :]).then_inc(gu_read, 1)

            act.wait_ge(zeros_in, 16)
            for n in range(4):
                shared_unit(2 * n)
                act.wait_ge(rot_ready, n + 1)
                act.wait_ge(parts_stored[n], 16)
                s, c = UP[n]
                piece(4 + n, 0, plain[:, s, c * HALF:(c + 1) * HALF]).then_inc(high_ready, 1)
                if n == 3:
                    for i in range(2):
                        nc.scalar.copy(token_act[:, i:i + 1], lat_bias[:, :]).then_inc(probs_ready, 1)
                    act.wait_ge(negmax_turned, 1)
                    nc.scalar.copy(negmax_rows[:, :], ps[0:48, 0, 0:64].bitcast(BF16)).then_inc(negmax_copied, 1)
                shared_unit(2 * n + 1)
                if n < 3:
                    middle(4 + n)
                    low(4 + n)

            def negmax_copy(m, c):
                act.wait_ge(negmax_turned, m + 1)
                act.wait_ge(negmax_in, 48 * m)
                nc.scalar.copy(negmax_rows[:, :], ps[0:48, 6 + c, 0:64].bitcast(BF16)).then_inc(negmax_copied, 1)

            def exps(g, c, kt):
                step = NT * (2 * g + c) + kt
                for j in range(GH):
                    act.wait_ge(scores_psum, GH * step + j + 1)
                    if j == 0:
                        act.wait_ge(probs_used, step + 1)
                    bank = j if isinstance(step, int) and step >= WIDE else j % 2
                    nc.scalar.activation(probs[:, kt % 2, j, :], ps[:, bank, :], ACT.Exp,
                                         scale=HD ** -0.5).then_inc(probs_ready, 1)

            def acc_copy(g, c, w):
                m = 2 * g + c
                act.wait_ge(probs_used, 2 + NT * (m + 1))
                act.wait_ge(scattered, 16 * NT)
                act.wait_ge(num_ready, 2 * (g // 2) + c + 1)
                act.wait_ge(den_ready, 2 * (g // 2) + c + 1)
                nc.scalar.activation(acc_sb[:, bass.ds(g % 2, 1), c, w, :].rearrange("p o t -> p (o t)"), ps[:, 6 + c, :],
                                     ACT.Copy, scale=rows_of[:, bass.ds(g % 2 + w, 1)]).then_inc(acc_read, 1)

            def half(g, c, last=False):
                for kt in range(LEAD, NT):
                    exps(g, c, kt)
                    if kt == 5 and not last:
                        negmax_copy(2 * g + c + 1, 1 - c)
                if last:
                    return
                for kt in range(LEAD):
                    exps(g + c, 1 - c, kt)
                    if kt < 2 and not (isinstance(g, int) and g == NG - 1):
                        acc_copy(g, c, kt)

            act.wait_ge(top_ready, 1)
            nc.scalar.activation(esc[:, :], top, ACT.Exp, scale=-1.0).then_inc(esc_ready, 1)
            act.wait_ge(hid_ready, 8)
            for kt in range(LEAD):
                exps(0, 0, kt)
                if kt == 0:
                    for i in range(2, 4):
                        nc.scalar.copy(token_act[:, i:i + 1], lat_bias[:, :]).then_inc(acc_read, 2)
                    middle(7)
                if kt == 1:
                    low(7)
            with act.Fori(0, NG - 1) as g:
                half(g, 0)
                half(g, 1)
            half(NG - 1, 0)
            half(NG - 1, 1, last=True)

            def evacuate(i):
                act.wait_ge(tile_gu_psum, i + 1)
                nc.scalar.activation(tile_gate, ps[:, 0, :], ACT.Silu).then_inc(tile_gate_ready, 1)

            def down_out(i):
                act.wait_ge(tile_y_psum, i + 1)
                if not isinstance(i, int) or i > 0:
                    act.wait_ge(tile_out, 16 * i)
                nc.scalar.copy(tile_y, ps[:, 5, 0:H]).then_inc(tile_y_ready, 1)
                act.wait_ge(tile_y_ready, i + 1)
                act.dma_start(sorted_y[bass.ds(i * P, P), :], tile_y).then_inc(tile_out, 16)

            def ht_copy(i):
                act.wait_ge(tile_ht_psum, i + 1)
                nc.scalar.copy(tile_ht, ps[:, 3, :].rearrange("p (k t) -> p k t", k=KF)).then_inc(tile_ht_ready, 1)

            evacuate(0)
            ht_copy(0)
            evacuate(1)
            down_out(0)
            ht_copy(1)
            with act.Fori(2, TILES) as i:
                evacuate(i)
                down_out(i - 1)
                ht_copy(i)
            down_out(TILES - 1)

        @block.vector
        def _(dve):
            nc.vector.memset(negmax_parts[:, :], 0.0).then_inc(casts_ready, 1)
            for hf in range(2):
                for t in range(4 * hf, 4 * hf + 4):
                    if t % 2 == 0:
                        dve.wait_ge(x_in[t // 2], 16)
                    nc.vector.bn_stats(stats[:, t, :], resid[:, t, :]).then_inc(stats_ready, 1)
                for t in range(4 * hf, 4 * hf + 4):
                    dve.wait_ge(stats_ready, t + 1)
                    nc.vector.bn_aggr(mv[:, t, :], stats[:, t, :]).then_inc(mv_ready, 1)
                dve.wait_ge(mv_ready, 4 * hf + 4)
                nc.vector.tensor_scalar(veps[:, 4 * hf:4 * hf + 4], mv[:, 4 * hf:4 * hf + 4, 1], EPS, None,
                                        ALU.add).then_inc(veps_ready, 1)
            for hf in range(2):
                dve.wait_ge(rstd_ready, hf + 1)
                for t in range(4 * hf, 4 * hf + 4):
                    nc.vector.tensor_scalar(xn[:, t, :], resid[:, t, :], mv[:, t, 0:1], rstd[:, t:t + 1],
                                            ALU.subtract, ALU.mult).then_inc(xn_ready, 1)
            for hf in range(2):
                dve.wait_ge(xt_psum, 2 * hf + 2)
                nc.vector.tensor_copy(x_t[:, 1, hf * HALF:(hf + 1) * HALF], ps[:, 2 * hf + 1, :]).then_inc(xt_ready_v, 1)
            nc.vector.tensor_copy(ident_bf[:, :], ident).then_inc(casts_ready, 1)
            nc.vector.tensor_copy(before_bf[:, :], before).then_inc(casts_ready, 1)
            for n in range(5):
                if n < 4:
                    s, c = UP[n]
                    tt = slice(c * HALF, (c + 1) * HALF)
                    dve.wait_ge(high_ready, n + 1)
                    if n >= 2:
                        dve.wait_ge(mid_ready, n - 1)
                        dve.wait_ge(res2_ready, n - 1)
                    nc.vector.tensor_tensor(res1[n % 2], plain[:, s, tt], parts[:, s, 0, tt], ALU.subtract).then_inc(res1_ready, 1)
                if n >= 1:
                    s, c = UP[n - 1]
                    dve.wait_ge(mid_ready, n)
                    if n >= 3:
                        dve.wait_ge(low_ready, n - 2)
                    nc.vector.tensor_tensor(res2[(n - 1) % 2], res1[(n - 1) % 2],
                                            parts[:, s, 1, c * HALF:(c + 1) * HALF], ALU.subtract).then_inc(res2_ready, 1)
                if n == 2:
                    for c in range(2):
                        dve.wait_ge(lgt_psum, c + 1)
                        nc.vector.tensor_copy(logit_t[0:E, c * HALF:(c + 1) * HALF], ps[0:E, 2 + c, :]).then_inc(lgt_ready, 1)

            def swap_product(n):
                s, c = UP[n]
                tt = slice(c * HALF, (c + 1) * HALF)
                for lo in (0, 64):
                    nc.vector.tensor_tensor(rot_b[n][lo:lo + 64, :], plain[64 - lo:128 - lo, s, tt], sin_t[64 - lo:128 - lo, tt],
                                            ALU.mult).then_inc(swapped, 1)

            steps = 0

            def route(ins):
                nonlocal steps
                steps += 1
                ins.then_inc(route_step, 1)
                dve.wait_ge(route_step, steps)

            dve.wait_ge(lg_psum, NT)
            nc.vector.tensor_copy(lg, ps[:, 2, 0:NT * E].rearrange("p (t e) -> p t e", t=NT)).then_inc(lg_ready, 1)
            dve.wait_ge(lg_ready, 1)
            nc.vector.tensor_reduce(top, lg, AX.X, ALU.max).then_inc(top_ready, 1)
            dve.wait_ge(top_ready, 1)
            route(nc.vector.tensor_tensor(pick, lg, top.unsqueeze(2).to_broadcast([P, NT, E]), ALU.is_equal))
            route(nc.vector.tensor_tensor(pick2, pick, weight_of, ALU.mult))
            route(nc.vector.tensor_reduce(pickmax, pick2, AX.X, ALU.max))
            route(nc.vector.tensor_tensor(onehot, pick2, pickmax.unsqueeze(2).to_broadcast([P, NT, E]), ALU.is_equal))
            nc.vector.tensor_copy(onehot_bf, onehot.rearrange("p t e -> p (t e)")).then_inc(onehot_ready, 1)
            dve.wait_ge(rope_in, 32)
            swap_product(0)
            dve.wait_ge(vw_in, 48)
            dve.wait_ge(ones_ready, 2)
            for t in range(NT):
                if t == 4:
                    swap_product(1)
                    dve.wait_ge(rank_psum, 1)
                    nc.vector.tensor_copy(ranks.rearrange("p a t e -> p (a t e)"), ps[:, 3, 0:2 * NT * E]).then_inc(ranks_ready, 1)
                dve.wait_ge(v_psum, 2 * (t // 2) + 2)
                for r in range(2):
                    groups = "p (g r j d) -> p g r j d"
                    nc.vector.tensor_tensor(v_ones[:, r::2, t, :, r * HD:(r + 1) * HD],
                                            ps[:, V_BANKS[t // 2], (t % 2) * H:(t % 2) * H + H].rearrange(groups, r=2, j=GH, d=HD)[:, :, r],
                                            v_bias.rearrange(groups, r=2, j=GH, d=HD)[:, :, r], ALU.add).then_inc(v_ready, 1)

            swap_product(2)
            swap_product(3)
            dve.wait_ge(ranks_ready, 1)
            route(nc.vector.memset(passed[:, 0, :], 0.0))
            for t in range(NT):
                route(nc.vector.tensor_tensor(passed[:, t + 1, :], passed[:, t, :], ranks[:, 1, t, :], ALU.add))
            route(nc.vector.tensor_tensor(cmp3, passed[:, NT, :].unsqueeze(2).to_broadcast([P, E, E]), steps_128, ALU.is_gt))
            route(nc.vector.tensor_reduce(tiles_of, cmp3, AX.X, ALU.add))
            route(nc.vector.tensor_tensor(cmp3, tiles_of.unsqueeze(1).to_broadcast([P, E, E]), earlier, ALU.mult))
            route(nc.vector.tensor_reduce(start_of, cmp3, AX.X, ALU.add))
            route(nc.vector.tensor_tensor(end_of, start_of, tiles_of, ALU.add))
            route(nc.vector.tensor_tensor(cmpj, end_of.unsqueeze(1).to_broadcast([P, TILES, E]), tile_no, ALU.is_le))
            route(nc.vector.tensor_reduce(tile_exp, cmpj, AX.X, ALU.add))
            route(nc.vector.tensor_scalar(tile_exp_i[:, :], tile_exp, float(E - 1), None, ALU.min))
            route(nc.vector.tensor_tensor(pick, passed[:, 0:NT, :], ranks[:, 0, :, :], ALU.add))
            route(nc.vector.scalar_tensor_tensor(pick2, start_of.unsqueeze(1).to_broadcast([P, NT, E]), float(P),
                                                 pick, ALU.mult, ALU.add))
            route(nc.vector.tensor_tensor(pick, pick2, onehot, ALU.mult))
            route(nc.vector.tensor_reduce(dest, pick, AX.X, ALU.add))
            nc.vector.tensor_copy(dest_i[:, :], dest).then_inc(dest_ready, 1)

            def row_max(n, c, i):
                dve.wait_ge(max_scores, n + 1)
                nc.vector.tensor_reduce(negmax[:, c, i:i + 1], ps[:, 2 + 2 * (i % 2):4 + 2 * (i % 2), :], AX.XY,
                                        ALU.max, negate=True).then_inc(max_read, 1)

            def negmax_cut(m, c):
                src = negmax[:, c, :]
                dve.wait_ge(max_read, 16 * (m + 1))
                if m > 0:
                    dve.wait_ge(negmax_turned, m)
                nc.vector.tensor_copy(negmax_parts[:, 0:16], src).then_inc(split_step, 1)
                dve.wait_ge(split_step, 4 * m + 1)
                nc.vector.tensor_tensor(split1[:, :], src, negmax_parts[:, 0:16], ALU.subtract).then_inc(split_step, 1)
                dve.wait_ge(split_step, 4 * m + 2)
                nc.vector.tensor_copy(negmax_parts[:, 16:32], split1[:, :]).then_inc(split_step, 1)
                dve.wait_ge(split_step, 4 * m + 3)
                nc.vector.tensor_tensor(split2[:, :], split1[:, :], negmax_parts[:, 16:32], ALU.subtract).then_inc(split_step, 1)
                dve.wait_ge(split_step, 4 * m + 4)
                nc.vector.tensor_copy(negmax_parts[:, 32:48], split2[:, :]).then_inc(negmax_split, 1)

            for n in range(AHEAD):
                row_max(n, n // 16, n % 16)
                if n == 15:
                    negmax_cut(0, 0)
            dve.wait_ge(esc_ready, 1)
            route(nc.vector.tensor_scalar(esc1[:, :], esc[:, :], 1.0, None, ALU.add))
            nc.vector.reciprocal(score[:, :], esc1[:, :]).then_inc(score_ready, 1)

            def invert(k):
                dve.wait_ge(den_ready, 2 + k + 1)
                nc.vector.reciprocal(den[:, k, :], den[:, k, :]).then_inc(inverted, 1)
                dve.wait_ge(inverted, k + 1)
                if k >= 1:
                    dve.wait_ge(attn_ready, k)
                nc.vector.memset(wait_slot[:, :], 0.0)
                nc.vector.stream_shuffle(rden[:, :], den[:, k, :], [(i + HD) % STRIP for i in range(STRIP)]).then_inc(rden_ready, 1)

            def maxima(m, c, tiles):
                for i in tiles:
                    row_max(16 * m + i, c, i)

            def half(m, c, cut=False):
                maxima(m + 1, 1 - c, range(8, 16))
                if cut:
                    negmax_cut(m + 1, 1 - c)
                else:
                    dve.wait_ge(negmax_split, m + 1)
                maxima(m + 2, c, range(8))

            half(0, 0, cut=True)
            half(1, 1)
            with dve.Fori(1, NG - 1) as g:
                half(2 * g, 0)
                half(2 * g + 1, 1)
            maxima(2 * NG - 1, 1, range(8, 16))
            def acc_copy(m):
                c = m % 2
                dve.wait_ge(probs_used, 2 + NT * (m + 1))
                dve.wait_ge(num_ready, 2 + c + 1)
                dve.wait_ge(den_ready, 2 + c + 1)
                for w in range(2):
                    nc.vector.tensor_scalar(acc_sb[:, 1, c, w, :], ps[:, 6 + c, :], rows_of[:, 1 + w:2 + w], None, ALU.mult)\
                        .then_inc(acc_read, 1)

            invert(0)
            acc_copy(2 * NG - 2)
            invert(1)
            invert(2)

            def token_sum(t, done=token_summed):
                dve.wait_ge(token_psum, t + 1)
                nc.vector.tensor_tensor(resid[:, t, :], ps[:, 4 if t == 1 else 6 + t % 2, 0:H], resid[:, t, :], ALU.add).then_inc(done, 1)

            token_sum(0)

            def xt_copy(i):
                dve.wait_ge(tile_turned, i + 1)
                nc.vector.tensor_copy(tile_xt, ps[:, turn_bank(i), 0:H].rearrange("p (k t) -> p k t", k=KH)).then_inc(tile_xt_ready, 1)

            def gate_up_product(i):
                dve.wait_ge(tile_gate_ready, i + 1)
                nc.vector.tensor_tensor(tile_h, ps[:, 1, :], tile_gate, ALU.mult).then_inc(tile_h_ready, 1)

            def routed(i):
                dve.wait_ge(tile_gu_psum, i + 1)
                xt_copy(i + 1)
                gate_up_product(i)

            xt_copy(0)
            acc_copy(2 * NG - 1)
            routed(0)
            token_sum(1)
            invert(3)
            with dve.Fori(1, TILES - 1) as i:
                routed(i)
            gate_up_product(TILES - 1)
            def add_routed(t, done):
                dve.wait_ge(gathered_in[t], 16)
                nc.vector.tensor_tensor(resid[:, t, :], resid[:, t, :], gathered[:, t, :], ALU.add).then_inc(done, 1)

            token_sum(EARLY)
            for t in range(NT - 1):
                if t % 2 == 0:
                    token_sum(EARLY + 1 + t // 2)
                dve.wait_ge(token_summed, t + 1)
                add_routed(t, final_ready)
            add_routed(NT - 1, routed_added)
            dve.wait_ge(routed_added, 1)
            token_sum(NT - 1, final_ready)

        @block.gpsimd
        def _(pool):
            nc.gpsimd.memset(minus_half[:, :], -0.5).then_inc(half_set, 1)
            nc.gpsimd.memset(probs_w[:, 0:H], 0.0).then_inc(zero_set, 1)
            nc.gpsimd.memset(ones_bf[:, :], 1.0).then_inc(ones_ready, 1)
            pool.wait_ge(half_set, 1)
            for hf in range(2):
                pool.wait_ge(veps_ready, hf + 1)
                nc.gpsimd.tensor_tensor(rstd[:, 4 * hf:4 * hf + 4], veps[:, 4 * hf:4 * hf + 4],
                                        minus_half[:, 4 * hf:4 * hf + 4], ALU.pow).then_inc(rstd_ready, 1)
            nc.gpsimd.memset(v_ones[:, :, :, :, :], 1.0).then_inc(ones_ready, 1)
            pool.wait_ge(zero_set, 1)
            pool.dma_start(sorted_x.rearrange("(i p) d -> p i d", p=P),
                           probs_w[:, 0:H].unsqueeze(1).to_broadcast([P, TILES, H])).then_inc(zeros_in, 16)
            pool.wait_ge(vw_in, 48)
            pool.wait_ge(rope_in, 32)
            for t in range(NT):
                pool.wait_ge(xn_ready, t + 1)
                nc.gpsimd.tensor_tensor(resid[:, t, :], resid[:, t, :], out_bias, ALU.add).then_inc(bias_added, 1)
            def shared_unit(u):
                fc, c = u % 4, u // 4
                pool.wait_ge(gu_read, 2 * u + 2)
                nc.gpsimd.tensor_tensor(hid[:, fc, c * HALF:(c + 1) * HALF], sh_gate[u % 2], sh_up[u % 2], ALU.mult)\
                    .then_inc(hid_ready, 1)

            def rotate(n):
                s, c = UP[n]
                tt = slice(c * HALF, (c + 1) * HALF)
                pool.wait_ge(high_ready, n + 1)
                pool.wait_ge(swapped, 2 * n + 2)
                nc.gpsimd.tensor_tensor(plain[:, s, tt], plain[:, s, tt], cos_t[:, tt], ALU.mult).then_inc(rot_a_ready, 1)
                pool.wait_ge(rot_a_ready, n + 1)
                nc.gpsimd.tensor_tensor(plain[:, s, tt], plain[:, s, tt], rot_b[n], ALU.add).then_inc(rot_ready, 1)

            for n in range(4):
                s, c = UP[n]
                tt = slice(c * HALF, (c + 1) * HALF)
                rotate(n)
                shared_unit(2 * n)
                pool.wait_ge(high_ready, 5 + n)
                pool.wait_ge(mid_ready, 3 + n)
                pool.wait_ge(res2_ready, 3 + n)
                nc.gpsimd.tensor_tensor(res1[n % 2], plain[:, s, tt], parts[:, s, 0, tt], ALU.subtract).then_inc(res1_ready, 1)
                shared_unit(2 * n + 1)
                pool.wait_ge(mid_ready, 5 + n)
                pool.wait_ge(low_ready, 3 + n)
                nc.gpsimd.tensor_tensor(res2[n % 2], res1[n % 2], parts[:, s, 1, tt], ALU.subtract).then_inc(res2_ready, 1)
            pool.wait_ge(score_ready, 1)
            pool.wait_ge(xt_psum, 4)
            for t in range(NT):
                nc.gpsimd.tensor_scalar(xn[:, t, :], xn[:, t, :], score[:, t:t + 1], None, ALU.mult).then_inc(scaled_ready, 1)
            pool.wait_ge(zeros_in, 16)
            nc.gpsimd.memset(token_pool[:, 0:1], 0.0).then_inc(num_ready, 2)
            nc.gpsimd.memset(token_pool[:, 1:2], 0.0).then_inc(den_ready, 2)
            pool.wait_ge(dest_ready, 1)
            pool.wait_ge(scaled_ready, NT)
            for t in range(NT):
                pool.indirect_dma_start(out=sorted_x[:, :], out_offset=bass.IndirectOffsetOnAxis(ap=dest_i[:, t:t + 1], axis=0),
                                        in_=xn[:, t, :], in_offset=None).then_inc(scattered, 16)

            def merge(k):
                r, c = k // 2, k % 2
                pool.wait_ge(acc_read, 2 * (2 + 4 * r + 2 + c + 1))
                nc.gpsimd.tensor_tensor(den[:, k, :], acc_sb[:, 0, c, 1, :], acc_sb[:, 1, c, 1, :], ALU.add).then_inc(den_ready, 1)
                nc.gpsimd.tensor_tensor(attn[:, r, c * HALF:(c + 1) * HALF], acc_sb[:, 0, c, 0, :], acc_sb[:, 1, c, 0, :],
                                        ALU.add).then_inc(num_ready, 1)

            def quotient(k):
                rows = attn[:, k // 2, k % 2 * HALF:(k % 2 + 1) * HALF]
                pool.wait_ge(num_ready, 2 + k + 1)
                pool.wait_ge(rden_ready, k + 1)
                nc.gpsimd.tensor_tensor(rows, rows, rden[:, :], ALU.mult).then_inc(attn_ready, 1)

            def negmax_cut(m, c):
                src = negmax[:, c, :]
                pool.wait_ge(max_read, 16 * (m + 1))
                pool.wait_ge(negmax_turned, m)
                nc.gpsimd.tensor_copy(negmax_parts[:, 0:16], src).then_inc(split_step, 1)
                pool.wait_ge(split_step, 4 * m + 1)
                nc.gpsimd.tensor_tensor(split1[:, :], src, negmax_parts[:, 0:16], ALU.subtract).then_inc(split_step, 1)
                pool.wait_ge(split_step, 4 * m + 2)
                nc.gpsimd.tensor_copy(negmax_parts[:, 16:32], split1[:, :]).then_inc(split_step, 1)
                pool.wait_ge(split_step, 4 * m + 3)
                nc.gpsimd.tensor_tensor(split2[:, :], split1[:, :], negmax_parts[:, 16:32], ALU.subtract).then_inc(split_step, 1)
                pool.wait_ge(split_step, 4 * m + 4)
                nc.gpsimd.tensor_copy(negmax_parts[:, 32:48], split2[:, :]).then_inc(negmax_split, 1)

            for m in range(2, 2 * NG):
                negmax_cut(m, m % 2)
                if m in (3, 4):
                    merge(m - 3)
            quotient(0)
            merge(2)
            quotient(1)
            quotient(2)
            merge(3)
            quotient(3)

            pool.wait_ge(tile_out, 16 * TILES)
            for t in range(NT):
                pool.indirect_dma_start(out=gathered[:, t, :], out_offset=None, in_=sorted_y[:, :],
                                        in_offset=bass.IndirectOffsetOnAxis(ap=dest_i[:, t:t + 1], axis=0)).then_inc(gathered_in[t], 16)

        @block.tensor
        def _(pe):
            pe.wait_ge(ones_ready, 1)
            for _ in range(WARM_UP):
                pe.matmul(ps[:, 7, :], ones_bf[:, :], ones_bf[:, :].unsqueeze(1).to_broadcast([P, 4, P]), start=True, stop=True)
            pe.wait_ge(consts_in, 16)
            for hf in range(2):
                pe.wait_ge(xn_ready, 4 * hf + 4)
                for k in range(KH):
                    for t in range(4):
                        last = pe.transpose(ps[:, 2 * hf + k, t * P:(t + 1) * P], xn[:, 4 * hf + t, k::KH], ident)
                    last.then_inc(xt_psum, 1)
            pe.wait_ge(latw_in, 32)
            for c in range(2):
                pe.wait_ge(xt_ready_a, c + 1)
                pe.wait_ge(xt_ready_v, c + 1)
                for k in range(KH):
                    last = pe.matmul(ps[:, 4 + c, :], lat_wt[:, k, :], x_t[:, k, c * HALF:(c + 1) * HALF],
                                     start=(k == 0), stop=(k == KH - 1))
                last.then_inc(lat_psum, 1)
            pe.wait_ge(upw_in, 48)
            for n in range(4):
                s, c = UP[n]
                pe.wait_ge(lat_ready, c + 1)
                pe.matmul(ps[:, (6 + n) % 8, :], up_wt[:, s * P:(s + 1) * P], lat[:, c * HALF:(c + 1) * HALF],
                          start=True, stop=True).then_inc(up_psum, 1)

            pe.wait_ge(router_in, 16)
            for c in range(2):
                for k in range(KH):
                    last = pe.matmul(ps[0:E, 2 + c, :], router_t[:, k, :], x_t[:, k, c * HALF:(c + 1) * HALF],
                                     start=(k == 0), stop=(k == KH - 1))
                last.then_inc(lgt_psum, 1)

            def v_tile(t):
                pe.matmul(ps[:, V_BANKS[t // 2], (t % 2) * H:(t % 2) * H + H], lat[:, t * P:(t + 1) * P], v_wt,
                          start=True, stop=True).then_inc(v_psum, 1)

            pe.wait_ge(vw_in, 48)
            for t in range(4):
                v_tile(t)
            pe.wait_ge(lgt_ready, 2)
            for t in range(NT):
                pe.transpose(ps[:, 2, t * E:(t + 1) * E], logit_t[0:E, t * P:(t + 1) * P], ident[0:E, 0:E]).then_inc(lg_psum, 1)

            def max_tile(n):
                c, g, j, qt = n // 16 % 2, n // 32, n % 16 // 4, n % 4
                if n % 16 == 0:
                    pe.wait_ge(stacks_in[g][c], 16 * STACK_LOADS[c])
                if n >= 2:
                    pe.wait_ge(max_read, n - 1)
                for kh in range(2):
                    last = pe.matmul(ps[:, 2 + 2 * (n % 2) + kh, :],
                                     q_stack[0:KROWS, g, c, j, qt * P:(qt + 1) * P],
                                     k_stack[0:KROWS, g, j, kh * HALF:(kh + 1) * HALF], start=True, stop=True)
                last.then_inc(max_scores, 1)

            def negmax_turn(m, c, bank=None):
                pe.wait_ge(negmax_split, m + 1)
                pe.transpose(ps[:, 6 + c if bank is None else bank, 0:64].bitcast(BF16), negmax_parts[:, :], ident_bf[:, :]).then_inc(negmax_turned, 1)

            fc_units = [(u % 4, u // 4) for u in range(8)]
            maxima = iter(range(AHEAD))
            pe.wait_ge(sgu_in, 16)
            for u, (fc, c) in enumerate(fc_units):
                b = 0 if u % 2 == 0 else 6
                if u == 0:
                    pe.wait_ge(plain_ready, 4)
                if u == 4:
                    pe.wait_ge(v_ready, 2 * NT)
                if u >= 2:
                    pe.wait_ge(gu_read, 2 * (u - 1))
                for w in range(2):
                    for k in range(KH):
                        if (u, w, k) == (7, 1, 1):
                            pe.wait_ge(gu_read, 14)
                            negmax_turn(0, 0, 0)
                        last = pe.matmul(ps[:, b + w, :], sgu[:, k, w * F + fc:(w + 1) * F:KF],
                                         x_t[:, k, c * HALF:(c + 1) * HALF], start=(k == 0), stop=(k == KH - 1))
                        if u == 7 and k == 0:
                            last.then_inc(probs_used, 1)
                        if k == KH - 1 and w == 1:
                            last.then_inc(gu_psum, 1)
                        for _ in range(MAXIMA_AFTER[u][2 * w + k]):
                            max_tile(next(maxima))
                if u == 0:
                    pe.wait_ge(lg_ready, 1)
                    v_tile(4)
                    v_tile(5)
                    pe.wait_ge(onehot_ready, 1)
                    pe.wait_ge(casts_ready, 3)
                    pe.wait_ge(ones_ready, 2)
                    pe.matmul(ps[:, 3, 0:NT * E], before_bf[:, :], onehot_bf, start=True, stop=True)
                    pe.matmul(ps[:, 3, NT * E:2 * NT * E], ones_bf[:, :], onehot_bf, start=True, stop=True).then_inc(rank_psum, 1)
                if u == 1:
                    pe.wait_ge(ranks_ready, 1)
                    v_tile(6)
                    v_tile(7)
            for n in maxima:
                max_tile(n)
            pe.wait_ge(gu_read, 16)

            def score_tile(g, c, kt, j):
                step = NT * (2 * g + c) + kt
                n = GH * step + j
                bank = j if step >= WIDE else j % 2
                if step < WIDE or step == WIDE and j < 2:
                    pe.wait_ge(probs_ready, n + 1)
                elif step > WIDE:
                    pe.wait_ge(probs_ready, n - 1)
                elif j == 2:
                    pe.wait_ge(max_read, 2 * NG * 16 - 1)
                pe.matmul(ps[:, bank, :], k_stack[0:ROWS, g, j, kt * P:(kt + 1) * P], q_stack[0:ROWS, g, c, j, :],
                          start=True, stop=True).then_inc(scores_psum, 1)

            def weigh(g, c, kt):
                step = NT * (2 * g + c) + kt
                pe.wait_ge(probs_ready, GH * step + GH + 2)
                for j in range(GH):
                    last = pe.matmul(ps[STRIP * j:STRIP * j + STRIP, 6 + c, :], v_ones[:, g, kt, j, :], probs[:, kt % 2, j, :],
                                     start=(kt == 0), stop=(kt == NT - 1))
                last.then_inc(probs_used, 1)

            maxima = iter(range(AHEAD, 2 * NG * 16))
            for m in range(2 * NG):
                g, c = m // 2, m % 2
                pe.wait_ge(negmax_in, 48 * (m + 1))
                for kt in range(NT):
                    score_tile(g, c, kt, 0)
                    score_tile(g, c, kt, 1)
                    wide = NT * m + kt > WIDE
                    if wide:
                        score_tile(g, c, kt, 2)
                        score_tile(g, c, kt, 3)
                    if kt == 1:
                        pe.wait_ge(acc_read, 2 * (m + 1))
                        pe.wait_ge(negmax_copied, m + 1)
                    if kt >= 1:
                        weigh(g, c, kt - 1)
                    elif m >= 1:
                        weigh((m - 1) // 2, 1 - c, NT - 1)
                    if not wide:
                        score_tile(g, c, kt, 2)
                        score_tile(g, c, kt, 3)
                    if kt == 5 and m + 1 < 2 * NG:
                        pe.wait_ge(acc_read, 2 * (m + 2))
                        negmax_turn(m + 1, 1 - c)
                    for n in (next(maxima, None), next(maxima, None)):
                        if n is not None:
                            max_tile(n)

            def token_tile(t):
                bank = 4 if t == 1 else 6 + t % 2
                if t == 3:
                    pe.wait_ge(acc_read, 2 * (2 + 2 * NG))
                if t >= 2:
                    pe.wait_ge(token_summed, t - 1)
                if t == T // 2 // P:
                    pe.wait_ge(attn_ready, 4)
                tt = slice(t * P, (t + 1) * P)
                for k in range(KF):
                    pe.matmul(ps[:, bank, 0:H], hid[:, k, tt], sdn[:, k, :], start=(k == 0), stop=False)
                for r in range(2):
                    last = pe.matmul(ps[:, bank, 0:H], attn[:, r, tt], wout[:, r, :], start=False, stop=(r == 1))
                last.then_inc(token_psum, 1)

            def turn_tile(i):
                pe.wait_ge(tile_in, 16 * (i + 1))
                for k in range(KH):
                    last = pe.transpose(ps[:, turn_bank(i), k * P:(k + 1) * P], tile_x[:, k::KH], ident)
                last.then_inc(tile_turned, 1)

            pe.wait_ge(tail_in, 32)
            pe.wait_ge(hid_ready, 8)
            pe.wait_ge(attn_ready, 3)
            pe.wait_ge(acc_read, 2 * (1 + 2 * NG))
            token_tile(0)
            turn_tile(0)
            weigh(NG - 1, 1, NT - 1)
            pe.wait_ge(probs_ready, 2 + 2 * NG * NT * GH)

            def expert_of(i):
                return pe.value_load(tile_exp_i[0:1, bass.ds(i, 1)], min_val=0, max_val=E - 1)

            def weights(e, at_, n):
                return exp_w[:, bass.ds(e, 1), at_:at_ + n].rearrange("p o n -> p (o n)")

            def gate_up_tile(i, e):
                pe.wait_ge(tile_xt_ready, i + 1)
                for w in range(2):
                    for k in range(KH):
                        last = pe.matmul(ps[:, w, :], tile_xt[:, k, :], weights(e, k * GU + w * F, F),
                                         start=(k == 0), stop=(k == KH - 1))
                last.then_inc(tile_gu_psum, 1)

            def turn_h(i):
                pe.wait_ge(tile_h_ready, i + 1)
                for k in range(KF):
                    last = pe.transpose(ps[:, 3, k * P:(k + 1) * P], tile_h[:, k::KF], ident)
                last.then_inc(tile_ht_psum, 1)

            def down_tile(i, e):
                pe.wait_ge(tile_ht_ready, i + 1)
                for k in range(KF):
                    last = pe.matmul(ps[:, 5, 0:H], tile_ht[:, k, :], weights(e, KH * GU + k * H, H),
                                     start=(k == 0), stop=(k == KF - 1))
                last.then_inc(tile_y_psum, 1)

            pe.wait_ge(exp_low_in, 16 * E)
            pe.wait_ge(exp_high_in, 16 * E)
            gate_up_tile(0, expert_of(0))
            turn_tile(1)
            token_tile(1)
            e_next = expert_of(1)
            turn_h(0)
            gate_up_tile(1, e_next)
            with pe.Fori(1, TILES - 1) as i:
                turn_tile(i + 1)
                down_tile(i - 1, expert_of(i - 1))
                e_next = expert_of(i + 1)
                turn_h(i)
                gate_up_tile(i + 1, e_next)
            pe.wait_ge(tile_y_ready, TILES - 2)
            down_tile(TILES - 2, expert_of(TILES - 2))
            turn_h(TILES - 1)
            token_tile(EARLY)
            pe.wait_ge(tile_y_ready, TILES - 1)
            down_tile(TILES - 1, expert_of(TILES - 1))
            for t in range(EARLY + 1, NT):
                token_tile(t)


def _constants():
    ident = np.eye(P, dtype=np.float32)
    before = np.triu(np.ones((P, P), np.float32), 1)
    weight_of = np.tile(np.arange(E, 0, -1, dtype=np.float32), NT)
    steps_128 = np.tile(P * np.arange(E, dtype=np.float32), E)
    earlier = np.tril(np.ones((E, E), np.float32), -1).reshape(-1)
    tile_no = np.repeat(np.arange(TILES, dtype=np.float32), E)
    row = np.concatenate([weight_of, steps_128, earlier, tile_no])
    first = (np.arange(P) % STRIP < HD).astype(np.float32)[:, None]
    return np.concatenate([ident, before, np.tile(row, (P, 1)), first, 1 - first, first], 1)


def _rope():
    dim = H // 4
    inv = (np.float32(1) / np.float32(10000.0) ** (np.arange(0, dim, 2, dtype=np.float32) / np.float32(dim))).astype(np.float32)
    freq = np.outer(np.arange(T, dtype=np.float32), inv).astype(np.float32).T
    cos, sin = np.cos(freq).astype(np.float32), np.sin(freq).astype(np.float32)
    return np.concatenate([cos] * 4), np.concatenate([sin, sin, -sin, -sin])


def kernel(**inputs):
    import concourse.bacc as bacc
    from concourse.bass_utils import run_bass_kernel_spmd

    a = {k.split("_", 1)[1]: np.asarray(v) for k, v in inputs.items()}
    wq, wk = a["attn_Wq_up"].T, a["attn_Wk_up"].T
    bq, bk = a["attn_bq_up"], a["attn_bk_up"]
    wo = a["attn_Wo"].T.reshape(2, 2, GH, HD, H).transpose(2, 1, 3, 0, 4)
    v_w = np.zeros((P, H), np.float32)
    v_w[64:] = a["attn_Wv_up"].T
    zero = np.zeros((LAT, P), np.float32)
    cos, sin = _rope()
    arrays = {
        "x": a["attn_hidden_states"].reshape(T, H),
        "lat_w": np.concatenate([a["attn_Wq_down"].T, a["attn_Wkv_down"].T], 1),
        "lat_b": np.concatenate([a["attn_bq_down"], a["attn_bkv_down"]])[:, None],
        "up_w": np.concatenate([np.concatenate([wq, zero], 1), np.concatenate([zero, wk], 1)], 0),
        "up_b": np.stack([bq, bk], 1),
        "v_w": v_w,
        "v_b": a["attn_bv_up"],
        "rope_c": cos,
        "rope_s": sin,
        "router_w": a["ffn_router_w"].T,
        "sgu_w": np.concatenate([a["ffn_shared_gate_w"], a["ffn_shared_up_w"]], 1),
        "sdn_w": a["ffn_shared_down_w"],
        "out_w": wo.reshape(P, 2, H),
        "out_b": a["attn_bo"],
        "gate_up": a["ffn_gate_up_proj"],
        "down": a["ffn_down_proj"],
        "consts": _constants(),
        "one_rows": np.ones((ROWS - KROWS, NH, T), mybir.dt.np(BF16)),
    }
    nc = bacc.Bacc("TRN2", target_bir_lowering=False, num_devices=1)
    args = []
    for name, value in arrays.items():
        arrays[name] = np.ascontiguousarray(value)
        args.append(nc.dram_tensor(name, arrays[name].shape, mybir.dt.from_np(arrays[name].dtype), kind="ExternalInput").ap())
    out = nc.dram_tensor("out", [T, H], F32, kind="ExternalOutput").ap()
    build_kernel(nc, *args, out)
    result = run_bass_kernel_spmd(nc, [arrays], core_ids=[0])
    return result.results[0]["out"].reshape(1, T, H)
```
